# Optimizing a Trainium2 kernel written in Bass

```python
import numpy as np
import jax
import jax.numpy as jnp

def _softmax(x, axis=-1):
    return jax.nn.softmax(x, axis=axis)

def _gelu(x):
    return jax.nn.gelu(x, approximate=True)

def _silu(x):
    return jax.nn.silu(x)

def _sigmoid(x):
    return jax.nn.sigmoid(x)

def _layernorm(x, axis=-1, eps=1e-05):
    m = jnp.mean(x, axis=axis, keepdims=True)
    v = jnp.var(x, axis=axis, keepdims=True)
    return (x - m) / jnp.sqrt(v + eps)

def _scatter_add(tgt, idx, src, axis=0):
    return tgt.at[idx].add(src)

def _segment_sum(src, seg, n):
    return jax.ops.segment_sum(src, seg, n)
kernel_name = 'mk_cond_resid_d1_seqx_r2_8d1098'

def setup_inputs(seed: int=0):
    np.random.seed(seed)
    _w = jnp.asarray

    def _rec_inputs():
        import jax
        import jax.numpy as jnp
        _rk = jax.random.key(seed)
        x = -0.0003929 + 0.9999 * jax.random.normal(jax.random.fold_in(_rk, 1), (64, 128, 2048), jnp.float32)
        _lenS = 128 - jax.random.randint(jax.random.fold_in(_rk, 7), (64,), 0, max(1, 128 // 4) + 1, jnp.int32)
        _lenS2 = 128 - jax.random.randint(jax.random.fold_in(_rk, 8), (64,), 0, max(1, 128 // 4) + 1, jnp.int32)
        itok_B_8_3872 = jax.random.randint(jax.random.fold_in(_rk, 11), (64,), 8, 3873, jnp.int32)
        return (x, itok_B_8_3872)
    x, itok_B_8_3872 = _rec_inputs()

    def _L0_cond_setup():
        import math
        import jax, jax.numpy as jnp
        import numpy as np
        H, N, B, L = (128, 64, 16, 2048)
        DT_MIN, DT_MAX = (0.001, 0.1)

        def _get_kernel(log_dt, C, log_A_real, A_imag, length):
            Cc = C[..., 0] + 1j * C[..., 1]
            dt = jnp.exp(log_dt)
            A = -jnp.exp(log_A_real) + 1j * A_imag
            dtA = A * dt[:, None]
            P = dtA[:, :, None] * jnp.arange(length, dtype=jnp.float32)
            Cs = Cc * (jnp.exp(dtA) - 1.0) / A
            K = 2.0 * jnp.einsum('hn,hnl->hl', Cs, jnp.exp(P)).real
            return K
        key = jax.random.key(seed)
        ks = jax.random.split(key, 6)
        u = jax.random.normal(ks[0], (B, H, L), dtype=jnp.float32)
        length = jax.random.randint(ks[1], (B,), 0, L)
        log_dt = jax.random.uniform(ks[2], (H,), dtype=jnp.float32) * (math.log(DT_MAX) - math.log(DT_MIN)) + math.log(DT_MIN)
        C = jax.random.normal(ks[3], (H, N, 2), dtype=jnp.float32)
        log_A_real = jnp.log(0.5 * jnp.ones((H, N), dtype=jnp.float32))
        A_imag = math.pi * jnp.broadcast_to(jnp.arange(N, dtype=jnp.float32), (H, N))
        D = jax.random.normal(ks[4], (H,), dtype=jnp.float32)
        return {'u': u, 'length': length, 'log_dt': log_dt, 'C': C, 'log_A_real': log_A_real, 'A_imag': A_imag, 'D': D}
    _L0_cond_all = _L0_cond_setup()
    _L0_cond_in = {k: v for k, v in _L0_cond_all.items() if k in ('log_dt', 'C', 'log_A_real', 'A_imag', 'D')}
    del _L0_cond_all
    return {'x': x, 'itok_B_8_3872': itok_B_8_3872, 'L0_cond_log_dt': _L0_cond_in['log_dt'], 'L0_cond_C': _L0_cond_in['C'], 'L0_cond_log_A_real': _L0_cond_in['log_A_real'], 'L0_cond_A_imag': _L0_cond_in['A_imag'], 'L0_cond_D': _L0_cond_in['D']}

def reference(x, itok_B_8_3872, L0_cond_log_dt, L0_cond_C, L0_cond_log_A_real, L0_cond_A_imag, L0_cond_D):
    import jax
    import jax.numpy as jnp

    def _L0_cond_ref(u, length, log_dt, C, log_A_real, A_imag, D):
        import math
        import jax, jax.numpy as jnp
        import numpy as np
        H, N, B, L = (128, 64, 16, 2048)
        DT_MIN, DT_MAX = (0.001, 0.1)

        def _get_kernel(log_dt, C, log_A_real, A_imag, length):
            Cc = C[..., 0] + 1j * C[..., 1]
            dt = jnp.exp(log_dt)
            A = -jnp.exp(log_A_real) + 1j * A_imag
            dtA = A * dt[:, None]
            P = dtA[:, :, None] * jnp.arange(length, dtype=jnp.float32)
            Cs = Cc * (jnp.exp(dtA) - 1.0) / A
            K = 2.0 * jnp.einsum('hn,hnl->hl', Cs, jnp.exp(P)).real
            return K
        Bq, Hq, Lq = u.shape
        mask = (jnp.arange(Lq) < length[:, None]).astype(u.dtype)
        u_m = u * mask[:, None, :]
        kernel = _get_kernel(log_dt, C, log_A_real, A_imag, Lq)
        n = 2 * Lq
        k_f = jnp.fft.rfft(kernel, n=n)
        u_f = jnp.fft.rfft(u_m, n=n)
        y = jnp.fft.irfft(u_f * k_f, n=n)[..., :Lq]
        y = y + u_m * D[:, None]
        return y * mask[:, None, :]
    x = x + _L0_cond_ref(x, itok_B_8_3872, L0_cond_log_dt, L0_cond_C, L0_cond_log_A_real, L0_cond_A_imag, L0_cond_D)
    return x

_drawn_inputs = setup_inputs


def setup_inputs(seed=0):
    import zlib

    import numpy as np

    out = dict(_drawn_inputs(seed))
    spreads = {'L0_cond_log_A_real': (-0.6931471824645996, 0.2)}
    factors = {}
    for name, (base, spread) in spreads.items():
        noise = np.random.default_rng([zlib.crc32(name.encode()), seed]).standard_normal(out[name].shape)
        drawn = base * np.exp(spread * noise) if base else spread * noise
        out[name] = jnp.asarray(drawn.astype(out[name].dtype))
    for name, factor in factors.items():
        out[name] = (out[name] * factor).astype(out[name].dtype)
    return out
```

```python
import math
from contextlib import ExitStack

import concourse.bass as bass
from concourse import mybir

ALU = mybir.AluOpType
ACT = mybir.ActivationFunctionType
F32 = mybir.dt.float32
F32R = mybir.dt.float32r
I32 = mybir.dt.int32

B, H, L, N = 64, 128, 2048, 64
P = 128
BLK = 128
CHUNK = 2 * BLK
HALF = L // 2
CPH = HALF // CHUNK
NC = 2 * CPH
SQ = 16
SLOTS = 4
GROUPS = H // SLOTS
KROW = 384
PAD = BLK - 1
POWERS = [2 ** k for k in range(11)]
NPOW = len(POWERS)
ZCOLS = [(1, 7), (2, 6), (3, 5), (5, 8)]
HOPS = [(1, 7, 1), (1, 6, 2), (0, 4, 4)]

S_X1, S_X2, S_Y1, S_Y2, S_R = 16, 17, 18, 19, 20
NSPEC = 26


def s4d_kernel(nc, x, length, log_dt, C, log_A_real, A_imag, D, out):
    ctx = ExitStack()
    with ctx:
        def sb(name, shape, dt=F32):
            return ctx.enter_context(nc.sbuf_tensor(name, shape, dt))

        def sem(name):
            return ctx.enter_context(nc.semaphore(name))

        krows = nc.dram_tensor("krows", [H, KROW], F32)

        prm = sb("prm", [P, 1 + N])
        cin = sb("cin", [P, 2 * N])
        aim = sb("aim", [P, N])
        drow = sb("drow", [1, H])
        ilen = sb("ilen", [P, 1], I32)
        flen = sb("flen", [P, 1])
        ex0 = sb("ex0", [P, 1 + N])
        wide = sb("wide", [P, 3 * NPOW * N])
        em1 = sb("em1", [P, N])
        cs = sb("cs", [P, 8, N])
        nat = sb("nat", [P, NSPEC, P])
        spec = sb("spec", [P, NSPEC, H])
        ident = sb("ident", [P, P])
        dmask = sb("dmask", [P, N])
        W1 = sb("W1", [P, 2, H, SQ])
        W2 = sb("W2", [P, 2, H, SQ])
        B1 = sb("B1", [P, 2, H, SQ])
        B2 = sb("B2", [P, 2, H, SQ])
        q1 = sb("q1", [P, H * 8])
        q2 = sb("q2", [P, H * 8])
        q3 = sb("q3", [P, H * 8])
        q4 = sb("q4", [P, H * 8])
        RV = sb("RV", [P, H, 12])
        bsel = sb("bsel", [P, H, SQ])
        onei = sb("onei", [1, 8, SQ])
        zpad = sb("zpad", [P, PAD + 2])
        mask = sb("mask", [P, HALF], I32)
        xs = [sb(f"xs{i}", [P, HALF]) for i in range(SLOTS)]
        uhi = [sb(f"uhi{i}", [P, NC * B], F32R) for i in range(2)]
        ulo = [sb(f"ulo{i}", [P, NC * B], F32R) for i in range(2)]
        uod = [sb(f"uod{i}", [P, NC * B]) for i in range(2)]
        zhi = [sb(f"zhi{i}", [P, NC * B], F32R) for i in range(2)]
        zlo = [sb(f"zlo{i}", [P, NC * B], F32R) for i in range(2)]
        ehi = [sb(f"ehi{i}", [P, P], F32R) for i in range(2)]
        elo = [sb(f"elo{i}", [P, P], F32R) for i in range(2)]
        eod = [sb(f"eod{i}", [P, P]) for i in range(2)]
        rot = [sb(f"rot{i}", [P, 12, N], F32R) for i in range(2)]
        tw1 = sb("tw1", [P, 2, SQ, SQ])
        tw2 = sb("tw2", [P, 2, SQ, SQ])
        pf = [sb(f"pf{i}", [P, 2, CHUNK]) for i in range(2)]
        fhi = [sb(f"fhi{i}", [P, CHUNK], F32R) for i in range(2)]
        flo = [sb(f"flo{i}", [P, CHUNK], F32R) for i in range(2)]
        traw = [sb(f"traw{i}", [P, CHUNK]) for i in range(2)]
        thi = [sb(f"thi{i}", [P, CHUNK], F32R) for i in range(2)]
        tlo = [sb(f"tlo{i}", [P, CHUNK], F32R) for i in range(2)]

        npn = NPOW * N

        def view(t, a=0):
            return t[:, a:a + npn].rearrange("p (k n) -> p k n", n=N)
        ta, tb, tc_, arg = q1[:, 0:npn], q2[:, 0:npn], q3[:, 0:npn], view(q4)
        mag, lre = view(xs[2]), view(xs[3])
        flatb = bsel[:].rearrange("p h i -> p (h i)")
        sn, sh = view(flatb), view(flatb, npn)
        ang, lim = view(wide), view(wide, npn)
        ti = wide[:, 2 * npn:3 * npn].bitcast(I32)
        dexp = wide[0:1, 0:H * SQ].rearrange("p (h i) -> p h i", i=SQ)
        ksb = nat[:, 0:SQ, :]

        def bank(name):
            return ctx.enter_context(nc.psum_tensor(name, [P, 512], F32))
        xt = [bank("xt_even"), bank("xt_odd")]
        vb = bank("vb")
        tab = bank("tab")
        yb = [[bank(f"y{i}{k}") for k in range(2)] for i in range(2)]
        pro = [xt[0], xt[1], vb, tab, yb[0][0], yb[0][1], yb[1][0]]

        s_prm = sem("s_prm")
        s_len = sem("s_len")
        s_pool0 = sem("s_pool0")
        s_dve = sem("s_dve")
        s_gp = sem("s_gp")
        s_ang = sem("s_ang")
        s_sin = sem("s_sin")
        s_nat = sem("s_nat")
        s_turn = sem("s_turn")
        s_spec = sem("s_spec")
        s_btab = sem("s_btab")
        s_tabs = sem("s_tabs")
        s_k = sem("s_k")
        s_ksb = sem("s_ksb")
        s_gpa = sem("s_gpa")
        s_kz = sem("s_kz")
        s_kd = sem("s_kd")
        s_x = [sem(f"s_x{i}") for i in range(SLOTS)]
        s_out = [sem(f"s_out{i}") for i in range(SLOTS)]
        s_t = [sem(f"s_t{i}") for i in range(2)]
        s_tr = sem("s_tr")
        s_et = sem("s_et")
        s_in = sem("s_in")
        s_l = sem("s_l")
        s_intra = sem("s_intra")
        s_y = sem("s_y")
        s_uhi = sem("s_uhi")
        s_uod = sem("s_uod")
        s_ulo = sem("s_ulo")
        s_zhi = sem("s_zhi")
        s_zlo = sem("s_zlo")
        s_ehi = sem("s_ehi")
        s_elo = sem("s_elo")
        s_fhi = sem("s_fhi")
        s_flo = sem("s_flo")
        s_thi = sem("s_thi")
        s_tlo = sem("s_tlo")
        s_pred = sem("s_pred")
        s_pf = sem("s_pf")
        s_r = sem("s_r")

        x_v = x.rearrange("b h (m f t) -> h f b m t", f=2, t=CHUNK)
        o_v = out.rearrange("b h (m f t) -> h f b m t", f=2, t=CHUNK)

        def groups(eng, body):
            for j in range(SLOTS):
                body(0, j)
            with eng.Fori(1, GROUPS - 1) as g:
                for j in range(SLOTS):
                    body(g, j)
            for j in range(SLOTS):
                body(GROUPS - 1, j)

        def forward(t):
            return t[:, 1, :].rearrange("p (i j) -> p i j", j=SQ)[:, ::-1, :]

        def three_d(t):
            return t[:].rearrange("p (i j) -> p i j", j=SQ)

        def chan(g, j):
            return g * SLOTS + j

        def is_last(g, j, ahead=1):
            return isinstance(g, int) and chan(g, j) + ahead >= H

        def is_first(g, j, back=1):
            return isinstance(g, int) and chan(g, j) < back

        def double(eng, link, t1, t2, part, back, first, ua, ub):
            m = 1
            for k in range(4):
                c = spec[:, 2 * (first + k), :].unsqueeze(2).broadcast_to([P, H, m])
                s = spec[:, 2 * (first + k) + 1, :].unsqueeze(2).broadcast_to([P, H, m])
                old = slice(SQ - m, SQ) if back else slice(0, m)
                new = slice(SQ - 2 * m, SQ - m) if back else slice(m, 2 * m)
                a = ua[:, 0:H * m].rearrange("p (h m) -> p h m", m=m)
                b = ub[:, 0:H * m].rearrange("p (h m) -> p h m", m=m)
                eng.tensor_tensor(a, t1[:, part, :, old], c, ALU.mult)
                link(eng.tensor_tensor(b, t2[:, part, :, old], s, ALU.mult))
                link(eng.tensor_tensor(t1[:, part, :, new], a, b, ALU.subtract))
                eng.tensor_tensor(a, t2[:, part, :, old], c, ALU.mult)
                link(eng.tensor_tensor(b, t1[:, part, :, old], s, ALU.mult))
                link(eng.tensor_tensor(t2[:, part, :, new], a, b, ALU.add))
                m *= 2

        block = ctx.enter_context(nc.Block())

        @block.sync
        def _(sp):
            sp.dma_start(prm[:, 0:1], log_dt.rearrange("(h a) -> h a", a=1)).then_inc(s_prm, 16)
            sp.dma_start(prm[:, 1:1 + N], log_A_real).then_inc(s_prm, 16)
            sp.dma_start(cin[:], C.rearrange("h n c -> h (n c)")).then_inc(s_prm, 16)
            sp.dma_start(aim[:], A_imag).then_inc(s_prm, 16)
            sp.dma_start(drow[:], D.rearrange("(a h) -> a h", a=1)).then_inc(s_prm, 16)
            for f in range(2):
                sp.dma_start(ilen[f * B:(f + 1) * B, :], length.rearrange("(b a) -> b a", a=1)).then_inc(s_len, 16)

            def load_x(g, j):
                for f in range(2):
                    sp.dma_start(xs[j][f * B:(f + 1) * B, :].rearrange("p (m t) -> p m t", t=CHUNK), x_v[chan(g, j), f]).then_inc(s_x[j], 16)

            def store(h, j):
                for f in range(2):
                    sp.dma_start(o_v[h, f], xs[j][f * B:(f + 1) * B, :].rearrange("p (m t) -> p m t", t=CHUNK)).then_inc(s_out[j], 16)

            def load_t(g, j):
                row = krows.ap()
                src = bass.AP(row.tensor, chan(g, j) * KROW, [[1, P], [1, CHUNK]])
                sp.dma_start(traw[j % 2][:], src).then_inc(s_t[j % 2], 16)

            for j in range(2):
                load_x(0, j)
            sp.wait_ge(s_pool0, 1)
            sp.dma_start(krows.ap()[:, CHUNK:CHUNK + PAD], zpad[:, 0:PAD]).then_inc(s_kz, 16)
            sp.wait_ge(s_ksb, 4)
            for c in range(8):
                dst = bass.AP(krows.ap().tensor, c * KROW, [[SQ, SQ], [8 * KROW, SQ], [1, SQ]])
                sp.dma_start(dst, ksb[c * SQ:(c + 1) * SQ, :, c * SQ:(c + 1) * SQ]).then_inc(s_kd, 16)
            sp.wait_ge(s_kz, 16)
            sp.wait_ge(s_kd, 16 * 8)
            for j in range(2):
                load_t(0, j)

            def channel(g, j):
                h = chan(g, j)
                if not is_first(g, j):
                    pj = (j - 1) % SLOTS
                    sp.wait_ge(s_pred, 2 * h)
                    store(h - 1, pj)
                if not is_last(g, j, 2):
                    if not is_first(g, j, 2):
                        k = (g if j >= 2 else g - 1)
                        sp.wait_ge(s_out[(j + 2) % SLOTS], 32 * (k + 1))
                    load_x(g + (j + 2) // SLOTS, (j + 2) % SLOTS)
                    sp.wait_ge(s_intra, h + 1)
                    load_t(g + (j + 2) // SLOTS, (j + 2) % SLOTS)

            groups(sp, channel)
            sp.wait_ge(s_pred, 2 * H)
            store(H - 1, SLOTS - 1)
            for j in range(SLOTS):
                sp.wait_ge(s_out[j], 32 * GROUPS)

        @block.gpsimd
        def _(pool):
            done = [0]

            def link(ins):
                done[0] += 1
                ins.then_inc(s_gp, 1)
                pool.wait_ge(s_gp, done[0])

            link(pool.memset(zpad[:], 0.0))
            link(pool.memset(ident[:], 0.0))
            link(pool.affine_select(out=ident[:], in_=ident[:], compare_op=ALU.not_equal, fill=1.0, base=0,
                                    pattern=[[-1, P]], channel_multiplier=1))
            link(pool.tensor_tensor(dmask[:], ident[:, 0:N], ident[:, N:2 * N], ALU.add))
            link(pool.memset(onei[:], 0.0))
            link(pool.memset(onei[:, :, SQ - 1:SQ], 1.0))
            link(pool.iota(mask[0:B, :], pattern=[[2 * CHUNK, CPH], [1, CHUNK]], base=0, channel_multiplier=0))
            link(pool.iota(mask[B:P, :], pattern=[[2 * CHUNK, CPH], [1, CHUNK]], base=CHUNK, channel_multiplier=0))
            pool.memset(B1[:, 1, :, 0:1], 1.0)
            pool.memset(B2[:, 1, :, 0:1], 0.0).then_inc(s_pool0, 1)
            pool.wait_ge(s_pool0, 1)

            pool.wait_ge(s_spec, 7)
            double(pool, link, B1, B2, 1, False, 0, q3, q4)
            link(pool.memset(dexp, 0.0))
            pool.wait_ge(s_prm, 16 * 5)
            pool.tensor_scalar(dexp[:, :, SQ - 1], drow[:], 1.0, None, ALU.add)
            pool.tensor_copy(B1[:, 0, :, :], B1[:, 1, :, ::-1])
            link(pool.tensor_copy(B2[:, 0, :, :], B2[:, 1, :, ::-1]))
            link(pool.tensor_copy(bsel[0:N], B1[0:N, 0, :, :]))
            pool.tensor_copy(bsel[N:P], B2[N:P, 0, :, :]).then_inc(s_btab, 1)
            pool.wait_ge(s_btab, 1)
            pool.wait_ge(s_tabs, 1)

            def channel(g, j):
                h, k = chan(g, j), j % 2
                if not is_first(g, j, 2):
                    pool.wait_ge(s_et, h - 1)
                    pool.wait_ge(s_flo, h - 1)
                w1 = W1[:, :, h].unsqueeze(3).broadcast_to([P, 2, SQ, SQ])
                w2 = W2[:, :, h].unsqueeze(3).broadcast_to([P, 2, SQ, SQ])
                b1 = B1[:, :, h].unsqueeze(2).broadcast_to([P, 2, SQ, SQ])
                b2 = B2[:, :, h].unsqueeze(2).broadcast_to([P, 2, SQ, SQ])
                if not is_first(g, j, 1):
                    pool.wait_ge(s_pf, h)
                pool.tensor_tensor(tw1[:], w1, b1, ALU.mult).then_inc(s_gpa, 1)
                pool.tensor_tensor(tw2[:], w2, b2, ALU.mult).then_inc(s_gpa, 1)
                pool.wait_ge(s_gpa, 2 * h + 2)
                pool.tensor_tensor(pf[k][:], tw1[:].rearrange("p a b c -> p a (b c)"),
                                   tw2[:].rearrange("p a b c -> p a (b c)"), ALU.subtract).then_inc(s_pf, 1)
                if not is_first(g, j, 2):
                    pool.wait_ge(s_l, 3 * h - 3)
                pool.tensor_tensor(rot[k][:], dmask[:].unsqueeze(1).broadcast_to([P, 12, N]),
                                   RV[:, h].unsqueeze(2).broadcast_to([P, 12, N]), ALU.mult).then_inc(s_r, 1)

            groups(pool, channel)

        @block.scalar
        def _(act):
            act.wait_ge(s_ang, 1)
            flat = ang.rearrange("p k n -> p (k n)")
            act.activation(sn.rearrange("p k n -> p (k n)"), flat, ACT.Sin)
            act.activation(sh.rearrange("p k n -> p (k n)"), flat, ACT.Sin, scale=0.5).then_inc(s_sin, 1)
            for q in range((NSPEC + 3) // 4):
                n = min(4, NSPEC - 4 * q)
                act.wait_ge(s_turn, q + 1)
                act.activation(spec[:, 4 * q:4 * q + n, :].rearrange("p a h -> p (a h)"), pro[q][:, 0:n * P],
                               ACT.Copy).then_inc(s_spec, 1)
            for q in range(4):
                act.wait_ge(s_k, q + 1)
                act.activation(ksb[:, 4 * q:4 * q + 4, :].rearrange("p a h -> p (a h)"), pro[q][:],
                               ACT.Copy).then_inc(s_ksb, 1)

            def turned(g, j):
                h, k = chan(g, j), j % 2
                act.wait_ge(s_tr, 2 * h + 1)
                act.activation(uhi[k][:], xt[0][:], ACT.Copy).then_inc(s_uhi, 1)
                act.wait_ge(s_tr, 2 * h + 2)
                act.activation(uod[k][:], xt[1][:], ACT.Copy).then_inc(s_uod, 1)

            def tables(g, j):
                h, k = chan(g, j), j % 2
                act.wait_ge(s_et, h + 1)
                act.activation(eod[k][:], tab[:, P:2 * P], ACT.Copy)
                act.activation(ehi[k][:], tab[:, 0:P], ACT.Copy).then_inc(s_ehi, 1)
                act.activation(three_d(fhi[k]), forward(pf[k]), ACT.Copy).then_inc(s_fhi, 1)
                act.wait_ge(s_t[k], 16 * (2 * g + j // 2 + 1))
                act.activation(thi[k][:], traw[k][:, ::-1], ACT.Copy).then_inc(s_thi, 1)

            def states(g, j, level):
                k = j % 2
                a, b = (B * c for c in ZCOLS[level])
                act.activation(zhi[k][:, a:b], vb[:, a:b], ACT.Copy).then_inc(s_zhi, 1)

            tables(0, 0)
            turned(0, 0)

            def channel(g, j):
                h = chan(g, j)
                nxt = (g + (j + 1) // SLOTS, (j + 1) % SLOTS)
                act.wait_ge(s_in, h + 1)
                states(g, j, 0)
                act.wait_ge(s_l, 3 * h + 1)
                states(g, j, 1)
                if not is_last(g, j):
                    tables(*nxt)
                act.wait_ge(s_l, 3 * h + 2)
                states(g, j, 2)
                act.wait_ge(s_l, 3 * h + 3)
                states(g, j, 3)
                if not is_last(g, j):
                    turned(*nxt)

            groups(act, channel)

        @block.vector
        def _(dve):
            done = [0]

            def link(ins):
                done[0] += 1
                ins.then_inc(s_dve, 1)
                dve.wait_ge(s_dve, done[0])

            LOG2E = 1.0 / math.log(2.0)
            LN2A = 0.693359375
            LN2B = math.log(2.0) - LN2A
            ROUND = 1.5 * 2.0 ** 23

            def exp(dst, src, n, minus1=None):
                k, r, q, i = ta[:, 0:n], tb[:, 0:n], tc_[:, 0:n], ti[:, 0:n]
                link(dve.tensor_scalar(r, src, -87.0, 87.0, ALU.max, ALU.min))
                link(dve.tensor_scalar(k, r, LOG2E, ROUND, ALU.mult, ALU.add))
                link(dve.tensor_scalar(k, k, ROUND, None, ALU.subtract))
                link(dve.scalar_tensor_tensor(out=r, in0=k, scalar=-LN2A, in1=r, op0=ALU.mult, op1=ALU.add))
                link(dve.scalar_tensor_tensor(out=r, in0=k, scalar=-LN2B, in1=r, op0=ALU.mult, op1=ALU.add))
                dve.tensor_scalar(i, k, 127.0, float(2 ** 23), ALU.add, ALU.mult)
                link(dve.tensor_scalar(q, r, 1.0 / math.factorial(7), None, ALU.mult))
                for d in range(6, 0, -1):
                    link(dve.scalar_tensor_tensor(out=q, in0=q, scalar=1.0 / math.factorial(d), in1=r,
                                                  op0=ALU.add, op1=ALU.mult))
                two_k = i.bitcast(F32)
                link(dve.scalar_tensor_tensor(out=dst, in0=q, scalar=1.0, in1=two_k, op0=ALU.add, op1=ALU.mult))
                if minus1 is not None:
                    m = minus1.shape[1]
                    link(dve.tensor_tensor(q[:, 0:m], q[:, 0:m], two_k[:, 0:m], ALU.mult))
                    link(dve.scalar_tensor_tensor(out=minus1, in0=two_k[:, 0:m], scalar=-1.0, in1=q[:, 0:m],
                                                  op0=ALU.add, op1=ALU.add))

            dve.wait_ge(s_prm, 16 * 5)
            exp(ex0[:], prm[:], 1 + N)
            dt = ex0[:, 0:1]
            link(dve.tensor_scalar(arg[:, 0, :], ex0[:, 1:1 + N], dt, -1.0, ALU.mult, ALU.mult))
            link(dve.tensor_scalar(ang[:, 0, :], aim[:], dt, None, ALU.mult))
            for k in range(1, NPOW):
                dve.tensor_scalar(arg[:, k, :], arg[:, 0, :], float(POWERS[k]), None, ALU.mult)
                ins = dve.tensor_scalar(ang[:, k, :], ang[:, 0, :], float(POWERS[k]), None, ALU.mult)
            link(ins)
            c1 = 6.28125
            c2 = round((2 * math.pi - c1) * 2 ** 21) / 2 ** 21
            c3 = 2 * math.pi - c1 - c2
            flat = ang.rearrange("p k n -> p (k n)")
            link(dve.tensor_scalar(ta, flat, 1.0 / (2 * math.pi), ROUND, ALU.mult, ALU.add))
            link(dve.tensor_scalar(ta, ta, ROUND, None, ALU.subtract))
            for c in (c1, c2, c3):
                link(dve.scalar_tensor_tensor(out=flat, in0=ta, scalar=-c, in1=flat, op0=ALU.mult, op1=ALU.add))
            link(dve.tensor_scalar(flat, flat, 3.1415925, -3.1415925, ALU.min, ALU.max))
            dve.tensor_copy(cs[:, 0, 0:1], ex0[:, 0:1]).then_inc(s_ang, 1)
            exp(mag.rearrange("p k n -> p (k n)"), arg.rearrange("p k n -> p (k n)"), NPOW * N, em1[:])
            dve.wait_ge(s_sin, 1)
            m, s, f = (t.rearrange("p k n -> p (k n)") for t in (mag, sh, sn))
            link(dve.scalar_tensor_tensor(out=ta, in0=s, scalar=-2.0, in1=s, op0=ALU.mult, op1=ALU.mult))
            dve.tensor_tensor(lim.rearrange("p k n -> p (k n)"), m, f, ALU.mult)
            link(dve.tensor_tensor(ta, m, ta, ALU.mult))
            link(dve.tensor_tensor(lre.rearrange("p k n -> p (k n)"), m, ta, ALU.add))
            l1r, l1i, n1, n2, dn, t1, cr, ci = (cs[:, i, :] for i in range(8))
            ar, ai = ex0[:, 1:1 + N], aim[:]
            link(dve.tensor_tensor(l1r, em1[:], ta[:, 0:N], ALU.add))
            l1i = lim[:, 0, :]
            dve.tensor_tensor(dn, ar, ar, ALU.mult)
            link(dve.tensor_tensor(t1, ai, ai, ALU.mult))
            link(dve.tensor_tensor(dn, dn, t1, ALU.add))
            link(dve.reciprocal(dn, dn))
            dve.tensor_tensor(n1, l1i, ai, ALU.mult)
            link(dve.tensor_tensor(t1, l1r, ar, ALU.mult))
            link(dve.tensor_tensor(n1, n1, t1, ALU.subtract))
            dve.tensor_tensor(n2, l1r, ai, ALU.mult)
            link(dve.tensor_tensor(t1, l1i, ar, ALU.mult))
            link(dve.scalar_tensor_tensor(out=n2, in0=n2, scalar=-1.0, in1=t1, op0=ALU.mult, op1=ALU.subtract))
            link(dve.tensor_tensor(n1, n1, dn, ALU.mult))
            link(dve.tensor_tensor(n2, n2, dn, ALU.mult))
            c_re = cin[:].rearrange("p (n c) -> p c n", c=2)[:, 0, :]
            c_im = cin[:].rearrange("p (n c) -> p c n", c=2)[:, 1, :]
            dve.tensor_tensor(cr, c_re, n1, ALU.mult)
            link(dve.tensor_tensor(t1, c_im, n2, ALU.mult))
            link(dve.tensor_tensor(cr, cr, t1, ALU.subtract))
            dve.tensor_tensor(ci, c_re, n2, ALU.mult)
            link(dve.tensor_tensor(t1, c_im, n1, ALU.mult))
            link(dve.tensor_tensor(ci, ci, t1, ALU.add))
            re, im = slice(0, N), slice(N, 2 * N)

            def put(row, part, src, factor=1.0):
                return dve.tensor_scalar(nat[:, row, part], src, factor, None, ALU.mult)

            for part in (re, im):
                dve.tensor_copy(nat[:, 0:16:2, part], lre[:, 0:8, :])
                dve.tensor_copy(nat[:, 1:16:2, part], lim[:, 0:8, :])
            put(S_X1, re, lre[:, 0, :])
            put(S_X1, im, lim[:, 0, :])
            put(S_X2, re, lim[:, 0, :])
            put(S_X2, im, lre[:, 0, :], -1.0)
            put(S_Y1, re, cr, 2.0)
            put(S_Y1, im, ci, -2.0)
            put(S_Y2, re, ci, 2.0)
            put(S_Y2, im, cr, 2.0)
            for q in range(3):
                put(S_R + 2 * q, re, lre[:, 8 + q, :])
                put(S_R + 2 * q, im, lim[:, 8 + q, :], -1.0)
                put(S_R + 2 * q + 1, re, lim[:, 8 + q, :])
                ins = put(S_R + 2 * q + 1, im, lre[:, 8 + q, :])
            ins.then_inc(s_nat, 1)
            dve.wait_ge(s_len, 32)
            link(dve.tensor_copy(flen[:], ilen[:]))
            dve.wait_ge(s_pool0, 1)
            link(dve.tensor_scalar(mask[:], mask[:], flen[:, 0:1], None, ALU.is_lt))
            for k in range(2):
                dve.memset(zhi[k][:, 0:B].bitcast(F32), 0.0)
                dve.memset(zlo[k][:, 0:B].bitcast(F32), 0.0)
            dve.wait_ge(s_spec, 7)
            dve.tensor_copy(W1[:, 0, :, SQ - 1], spec[:, S_X1, :])
            dve.tensor_copy(W2[:, 0, :, SQ - 1], spec[:, S_X2, :])
            dve.tensor_copy(W1[:, 1, :, SQ - 1], spec[:, S_Y1, :])
            link(dve.tensor_copy(W2[:, 1, :, SQ - 1], spec[:, S_Y2, :]))
            double(dve, link, W1, W2, 1, True, 4, q1, q2)
            double(dve, link, W1, W2, 0, True, 4, q1, q2)
            rv = RV[:].rearrange("p h (q l c) -> p q l c h", q=3, l=2)
            for q in range(3):
                link(dve.tensor_copy(rv[:, q, 0].bitcast(F32R), spec[:, S_R + 2 * q:S_R + 2 * q + 2, :]))
                link(dve.tensor_tensor(rv[:, q, 1], spec[:, S_R + 2 * q:S_R + 2 * q + 2, :], rv[:, q, 0],
                                       ALU.subtract))
            dve.tensor_copy(cs[:, 0, 0:1], ex0[:, 0:1]).then_inc(s_tabs, 1)

            def states(g, j, level):
                h, k = chan(g, j), j % 2
                a, b = (B * c for c in ZCOLS[level])
                dve.wait_ge(s_zhi, 4 * h + level + 1)
                dve.tensor_tensor(zlo[k][:, a:b], vb[:, a:b], zhi[k][:, a:b].bitcast(F32),
                                  ALU.subtract).then_inc(s_zlo, 1)

            def turned(g, j):
                h, k = chan(g, j), j % 2
                dve.wait_ge(s_uhi, h + 1)
                dve.tensor_tensor(ulo[k][:], xt[0][:], uhi[k][:].bitcast(F32), ALU.subtract).then_inc(s_ulo, 1)

            def tables(g, j):
                h, k = chan(g, j), j % 2
                dve.wait_ge(s_ehi, h + 1)
                dve.tensor_tensor(elo[k][:], tab[:, 0:P], ehi[k][:].bitcast(F32), ALU.subtract).then_inc(s_elo, 1)
                dve.wait_ge(s_fhi, h + 1)
                dve.tensor_tensor(three_d(flo[k]), forward(pf[k]), three_d(fhi[k]).bitcast(F32),
                                  ALU.subtract).then_inc(s_flo, 1)
                dve.wait_ge(s_thi, h + 1)
                dve.tensor_tensor(tlo[k][:], traw[k][:, ::-1], thi[k][:].bitcast(F32), ALU.subtract).then_inc(s_tlo, 1)

            def choose(g, j, part):
                a = part * 512
                dve.copy_predicated(xs[j][:, a:a + 512], mask[:, a:a + 512], yb[j % 2][part][:]).then_inc(s_pred, 1)

            tables(0, 0)
            turned(0, 0)

            def channel(g, j):
                h = chan(g, j)
                nxt = (g + (j + 1) // SLOTS, (j + 1) % SLOTS)
                prv = (g if j else g - 1, (j - 1) % SLOTS)
                if not is_first(g, j):
                    dve.wait_ge(s_y, 2 * h)
                states(g, j, 0)
                if not is_first(g, j):
                    choose(*prv, 0)
                states(g, j, 1)
                if not is_last(g, j):
                    tables(*nxt)
                states(g, j, 2)
                if not is_first(g, j):
                    choose(*prv, 1)
                states(g, j, 3)
                if not is_last(g, j):
                    turned(*nxt)

            groups(dve, channel)
            for part in range(2):
                dve.wait_ge(s_y, 2 * H - 1 + part)
                choose(GROUPS - 1, SLOTS - 1, part)

        @block.tensor
        def _(pe):
            pe.wait_ge(s_pool0, 1)
            pe.wait_ge(s_nat, 1)
            for q in range((NSPEC + 3) // 4):
                n = min(4, NSPEC - 4 * q)
                for r in range(n):
                    mm = pe.transpose(pro[q][:, r * P:(r + 1) * P], nat[:, 4 * q + r, :], ident[:])
                mm.then_inc(s_turn, 1)
            pe.wait_ge(s_spec, 7)
            pe.wait_ge(s_btab, 1)
            pe.wait_ge(s_tabs, 1)
            for g in range(H // 8):
                o = pro[g // 4][:, (g % 4) * P:(g % 4 + 1) * P]
                pe.matmul(o, W1[:, 1, 8 * g:8 * g + 8, :].rearrange("p c i -> p (c i)"), bsel[:, 8 * g:8 * g + 8, :].rearrange("p c i -> p (c i)"), start=True, stop=False)
                mm = pe.matmul(o, onei[:].rearrange("p c i -> p (c i)"),
                               dexp[:, 8 * g:8 * g + 8, :].rearrange("p c i -> p (c i)"), start=False, stop=True)
                if g % 4 == 3:
                    mm.then_inc(s_k, 1)

            def turn_x(g, j):
                h = chan(g, j)
                pe.wait_ge(s_x[j], 32 * (g + 1))
                for par in range(2):
                    for c in range(CPH):
                        b = 2 * c + par
                        mm = pe.transpose(xt[par][:, c * P:(c + 1) * P], xs[j][:, b * BLK:(b + 1) * BLK], ident[:])
                    mm.then_inc(s_tr, 1)

            def turn_e(g, j):
                h, k = chan(g, j), j % 2
                pe.wait_ge(s_pf, h + 1)
                pe.transpose(tab[:, 0:P], pf[k][:, 0, 0:P], ident[:])
                pe.transpose(tab[:, P:2 * P], pf[k][:, 0, P:2 * P], ident[:]).then_inc(s_et, 1)

            def three(o, a_hi, a_lo, b_hi, b_lo, start, stop):
                pe.matmul(o, a_hi, b_hi, start=start, stop=False, skip_group_check=True)
                pe.matmul(o, a_hi, b_lo, start=False, stop=False, skip_group_check=True)
                return pe.matmul(o, a_lo, b_hi, start=False, stop=stop, skip_group_check=True)

            def toeplitz(g, j, c):
                k = j % 2
                o = yb[k][c // 2][:, (c % 2) * CHUNK:(c % 2 + 1) * CHUNK]
                b = slice(c * P, (c + 1) * P)
                three(o, uhi[k][:, b], ulo[k][:, b], thi[k][:], tlo[k][:], c % 2 == 0, False)
                return pe.matmul(o[:, BLK:2 * BLK], uod[k][:, b], traw[k][:, :BLK - 1:-1], start=False, stop=False,
                                 skip_group_check=True)

            def hop(g, j, level):
                k = j % 2
                a, b, by = HOPS[level]
                w = [rot[k][:, 4 * level + 2 * i:4 * level + 2 * i + 2, :].rearrange("p c n -> p (c n)") for i in range(2)]
                cols = slice(B * a, B * b)
                three(vb[:, B * (a + by):B * (b + by)], w[0], w[1], zhi[k][:, cols], zlo[k][:, cols], False,
                      level == 2).then_inc(s_l, 1)

            pe.wait_ge(s_ksb, 4)
            turn_e(0, 0)
            turn_x(0, 0)

            def channel(g, j):
                h, k = chan(g, j), j % 2
                nxt = (g + (j + 1) // SLOTS, (j + 1) % SLOTS)
                pe.wait_ge(s_uod, h + 1)
                pe.wait_ge(s_ulo, h + 1)
                pe.wait_ge(s_elo, h + 1)
                if not is_first(g, j):
                    pe.wait_ge(s_zlo, 4 * h)
                cols = slice(0, (NC - 1) * B)
                o = vb[:, B:NC * B]

                three(o, ehi[k][:], elo[k][:], uhi[k][:, cols], ulo[k][:, cols], True, False)
                pe.matmul(o, eod[k][:], uod[k][:, cols], start=False, stop=False, skip_group_check=True).then_inc(s_in, 1)
                pe.wait_ge(s_tlo, h + 1)
                if not is_first(g, j, 2):
                    pe.wait_ge(s_pred, 2 * h - 2)
                toeplitz(g, j, 0)
                toeplitz(g, j, 1)
                pe.wait_ge(s_r, h + 1)
                pe.wait_ge(s_zlo, 4 * h + 1)
                hop(g, j, 0)
                toeplitz(g, j, 2)
                if not is_last(g, j):
                    turn_e(*nxt)
                pe.wait_ge(s_zlo, 4 * h + 2)
                hop(g, j, 1)
                toeplitz(g, j, 3).then_inc(s_intra, 1)
                pe.wait_ge(s_zlo, 4 * h + 3)
                hop(g, j, 2)
                if not is_last(g, j):
                    turn_x(*nxt)
                pe.wait_ge(s_flo, h + 1)
                pe.wait_ge(s_zlo, 4 * h + 4)
                for c in range(CPH):
                    b = slice(c * P, (c + 1) * P)
                    mm = three(yb[k][c // 2][:, (c % 2) * CHUNK:(c % 2 + 1) * CHUNK], zhi[k][:, b], zlo[k][:, b],
                               fhi[k][:], flo[k][:], False, c % 2 == 1)
                    if c % 2:
                        mm.then_inc(s_y, 1)

            groups(pe, channel)


_INS = ['x', 'itok_B_8_3872', 'L0_cond_log_dt', 'L0_cond_C', 'L0_cond_log_A_real', 'L0_cond_A_imag', 'L0_cond_D']


def kernel(**inputs):
    import numpy as _np
    import concourse.bacc as _bacc
    from concourse import mybir as _mybir
    from concourse.bass_utils import run_bass_kernel_spmd as _run

    nc = _bacc.Bacc("TRN2", target_bir_lowering=False, num_devices=1)
    arrays, args = {}, []
    for name in _INS:
        a = _np.ascontiguousarray(inputs[name])
        arrays[f"in_{name}_dram"] = a
        args.append(nc.dram_tensor(f"in_{name}_dram", a.shape, _mybir.dt.from_np(a.dtype), kind="ExternalInput").ap())
    out = nc.dram_tensor("out_0_dram", inputs["x"].shape, _mybir.dt.float32, kind="ExternalOutput").ap()
    s4d_kernel(nc, *args, out)
    r = _run(nc, [arrays], core_ids=[0])
    return r.results[0]["out_0_dram"]
```

```python
import math
from contextlib import ExitStack

import concourse.bass as bass
from concourse import mybir

ALU = mybir.AluOpType
ACT = mybir.ActivationFunctionType
F32 = mybir.dt.float32
F32R = mybir.dt.float32r
I32 = mybir.dt.int32

B, H, L, N = 64, 128, 2048, 64
P = 128
BLK = 128
CHUNK = 2 * BLK
HALF = L // 2
CPH = HALF // CHUNK
NC = 2 * CPH
SQ = 16
SLOTS = 6
GROUPS = H // SLOTS
KROW = 384
PAD = BLK - 1
POWERS = [2 ** k for k in range(11)]
NPOW = len(POWERS)
ZCOLS = [(1, 7), (2, 6), (3, 5), (5, 8)]
HOPS = [(1, 7, 1), (1, 6, 2), (0, 4, 4)]

S_X1, S_X2, S_Y1, S_Y2, S_R = 16, 17, 18, 19, 20
NSPEC = 26
XSPLIT = 32


def s4d_kernel(nc, x, length, log_dt, C, log_A_real, A_imag, D, out):
    ctx = ExitStack()
    with ctx:
        def sb(name, shape, dt=F32):
            return ctx.enter_context(nc.sbuf_tensor(name, shape, dt))

        def sem(name):
            return ctx.enter_context(nc.semaphore(name))

        krows = nc.dram_tensor("krows", [H, KROW], F32)

        prm = sb("prm", [P, 1 + N])
        cin = sb("cin", [P, 2 * N])
        aim = sb("aim", [P, N])
        dall = sb("dall", [P, H])
        dsel = sb("dsel", [P, 1])
        ilen = sb("ilen", [P, 1], I32)
        flen = sb("flen", [P, 1])
        ex0 = sb("ex0", [P, 1 + N])
        wide = sb("wide", [P, 3 * NPOW * N])
        em1 = sb("em1", [P, N])
        cs = sb("cs", [P, 8, N])
        nat = sb("nat", [P, NSPEC, P])
        spec = sb("spec", [P, NSPEC, H])
        ident = sb("ident", [P, P])
        dmask = sb("dmask", [P, N])
        W1 = sb("W1", [P, 2, H, SQ])
        W2 = sb("W2", [P, 2, H, SQ])
        B1 = sb("B1", [P, 1, H, SQ])
        B2 = sb("B2", [P, 1, H, SQ])
        q1 = sb("q1", [P, H * 8])
        q2 = sb("q2", [P, H * 8])
        q3 = sb("q3", [P, H * 8])
        q4 = sb("q4", [P, H * 8])
        RV = sb("RV", [P, H, 12])
        bsel = sb("bsel", [P, H, SQ])
        zpad = sb("zpad", [P, PAD + 2])
        mask = sb("mask", [P, HALF], I32)
        xs = [sb(f"xs{i}", [P, HALF]) for i in range(SLOTS)]
        uhi = [[sb(f"uhi{i}{p}", [P, NC * B], F32R) for p in range(2)] for i in range(2)]
        ulo = [[sb(f"ulo{i}{p}", [P, NC * B], F32R) for p in range(2)] for i in range(2)]
        uod = [sb(f"uod{i}", [P, NC * B]) for i in range(2)]
        zhi = [sb(f"zhi{i}", [P, NC * B], F32R) for i in range(2)]
        zlo = [sb(f"zlo{i}", [P, NC * B], F32R) for i in range(2)]
        ehi = [sb(f"ehi{i}", [P, 2 * P], F32R) for i in range(2)]
        elo = [sb(f"elo{i}", [P, 2 * P], F32R) for i in range(2)]
        rot = [sb(f"rot{i}", [P, 12, N], F32R) for i in range(2)]
        tw1 = sb("tw1", [P, 2, SQ, SQ])
        tw2 = sb("tw2", [P, 2, SQ, SQ])
        pf = [sb(f"pf{i}", [P, 2, CHUNK]) for i in range(2)]
        fhi = [sb(f"fhi{i}", [P, CHUNK], F32R) for i in range(2)]
        flo = [sb(f"flo{i}", [P, CHUNK], F32R) for i in range(2)]
        traw = [sb(f"traw{i}", [P, CHUNK]) for i in range(2)]
        thi = [sb(f"thi{i}", [P, CHUNK], F32R) for i in range(2)]
        tlo = [sb(f"tlo{i}", [P, CHUNK], F32R) for i in range(2)]

        npn = NPOW * N

        def view(t, a=0):
            return t[:, a:a + npn].rearrange("p (k n) -> p k n", n=N)
        ta, tb, tc_, arg = q1[:, 0:npn], q2[:, 0:npn], q3[:, 0:npn], view(q4)
        mag, lre = view(xs[4]), view(xs[5])
        flatb = bsel[:].rearrange("p h i -> p (h i)")
        sn, sh = view(flatb), view(flatb, npn)
        ang, lim = view(wide), view(wide, npn)
        ti = wide[:, 2 * npn:3 * npn].bitcast(I32)
        ksb = nat[:, 0:SQ, :]

        def bank(name):
            return ctx.enter_context(nc.psum_tensor(name, [P, 512], F32))
        xt = [bank("xt_even"), bank("xt_odd")]
        vb = [bank(f"v{i}") for i in range(2)]
        yb = [[bank(f"y{i}{k}") for k in range(2)] for i in range(2)]
        pro = [xt[0], xt[1], vb[0], vb[1], yb[0][0], yb[0][1], yb[1][0]]

        mexp = q4[:, 0:6 * N]
        kbank = [vb[0], vb[1], yb[0][0], yb[1][0]]

        s_prm = sem("s_prm")
        s_len = sem("s_len")
        s_pool0 = sem("s_pool0")
        s_dve = sem("s_dve")
        s_gp = sem("s_gp")
        s_ang = sem("s_ang")
        s_sin = sem("s_sin")
        s_lam = sem("s_lam")
        s_nata = sem("s_nata")
        s_nat = sem("s_nat")
        s_turn = sem("s_turn")
        s_spec = sem("s_spec")
        s_btab = sem("s_btab")
        s_xtab = sem("s_xtab")
        s_rhi = sem("s_rhi")
        s_kfin = sem("s_kfin")
        s_xini = sem("s_xini")
        s_ytab = sem("s_ytab")
        s_bsel = sem("s_bsel")
        s_tabs = sem("s_tabs")
        s_k = sem("s_k")
        s_ksb = sem("s_ksb")
        s_gpa = sem("s_gpa")
        s_kz = sem("s_kz")
        s_kd = sem("s_kd")
        s_x = [sem(f"s_x{i}") for i in range(SLOTS)]
        s_out = [sem(f"s_out{i}") for i in range(SLOTS)]
        s_t = [sem(f"s_t{i}") for i in range(2)]
        s_tr = sem("s_tr")
        s_et = sem("s_et")
        s_in = sem("s_in")
        s_l = sem("s_l")
        s_intra = sem("s_intra")
        s_y = sem("s_y")
        s_uhi = [sem(f"s_uhi{p}") for p in range(2)]
        s_ulo = [sem(f"s_ulo{p}") for p in range(2)]
        s_uod = sem("s_uod")
        s_zhi = sem("s_zhi")
        s_zlo = sem("s_zlo")
        s_ehi = sem("s_ehi")
        s_elo = sem("s_elo")
        s_fhi = sem("s_fhi")
        s_flo = sem("s_flo")
        s_thi = sem("s_thi")
        s_tlo = sem("s_tlo")
        s_pred = sem("s_pred")
        s_pf = sem("s_pf")
        s_r = sem("s_r")

        x_v = x.rearrange("b h (m f t) -> h f b m t", f=2, t=CHUNK)
        o_v = out.rearrange("b h (m f t) -> h f b m t", f=2, t=CHUNK)

        def groups(eng, body):
            for j in range(SLOTS):
                body(0, j)
            with eng.Fori(1, GROUPS - 1) as g:
                for j in range(SLOTS):
                    body(g, j)
            for h in range((GROUPS - 1) * SLOTS, H):
                body(h // SLOTS, h % SLOTS)

        rvl = RV[:].rearrange("p h (q l c) -> p q l c h", q=3, l=2)

        def e_bank(j):
            return yb[(j + 1) % 2][1][:, 0:2 * P]

        def on(g, j, d):
            return g + (j + d) // SLOTS, (j + d) % SLOTS

        def chan(g, j):
            return g * SLOTS + j

        def exists(g, j, d):
            return not isinstance(g, int) or 0 <= chan(g, j) + d < H

        def double(eng, link, t1, t2, part, first, ua, ub, lo=0, hi=H):
            m = 1
            for k in range(4):
                c = spec[:, 2 * (first + k), lo:hi].unsqueeze(2).broadcast_to([P, hi - lo, m])
                s = spec[:, 2 * (first + k) + 1, lo:hi].unsqueeze(2).broadcast_to([P, hi - lo, m])
                old = slice(SQ - m, SQ)
                new = slice(SQ - 2 * m, SQ - m)
                a = ua[:, 0:(hi - lo) * m].rearrange("p (h m) -> p h m", m=m)
                b = ub[:, 0:(hi - lo) * m].rearrange("p (h m) -> p h m", m=m)
                eng.tensor_tensor(a, t1[:, part, lo:hi, old], c, ALU.mult)
                link(eng.tensor_tensor(b, t2[:, part, lo:hi, old], s, ALU.mult))
                link(eng.tensor_tensor(t1[:, part, lo:hi, new], a, b, ALU.subtract))
                eng.tensor_tensor(a, t2[:, part, lo:hi, old], c, ALU.mult)
                link(eng.tensor_tensor(b, t1[:, part, lo:hi, old], s, ALU.mult))
                link(eng.tensor_tensor(t2[:, part, lo:hi, new], a, b, ALU.add))
                m *= 2

        block = ctx.enter_context(nc.Block())

        @block.sync
        def _(sp):
            sp.dma_start(prm[:, 0:1], log_dt.rearrange("(h a) -> h a", a=1)).then_inc(s_prm, 16)
            sp.dma_start(prm[:, 1:1 + N], log_A_real).then_inc(s_prm, 16)
            sp.dma_start(cin[:], C.rearrange("h n c -> h (n c)")).then_inc(s_prm, 16)
            sp.dma_start(aim[:], A_imag).then_inc(s_prm, 16)
            sp.dma_start(dall[:], D.rearrange("(a h) -> a h", a=1).broadcast_to([P, H])).then_inc(s_len, 16)
            for f in range(2):
                sp.dma_start(ilen[f * B:(f + 1) * B, :], length.rearrange("(b a) -> b a", a=1)).then_inc(s_len, 16)

            def load_x(g, j):
                for f in range(2):
                    sp.dma_start(xs[j][f * B:(f + 1) * B, :].rearrange("p (m t) -> p m t", t=CHUNK),
                                 x_v[chan(g, j), f]).then_inc(s_x[j], 16)

            def store(g, j):
                for f in range(2):
                    sp.dma_start(o_v[chan(g, j), f],
                                 xs[j][f * B:(f + 1) * B, :].rearrange("p (m t) -> p m t", t=CHUNK)).then_inc(s_out[j], 16)

            def load_t(g, j):
                src = bass.AP(krows.ap().tensor, chan(g, j) * KROW, [[1, P], [1, CHUNK]])
                sp.dma_start(traw[j % 2][:], src).then_inc(s_t[j % 2], 16)

            for j in range(3):
                load_x(0, j)
            sp.wait_ge(s_pool0, 1)
            sp.dma_start(krows.ap()[:, CHUNK:CHUNK + PAD], zpad[:, 0:PAD]).then_inc(s_kz, 16)
            sp.wait_ge(s_kfin, 1)
            for c in range(8):
                dst = bass.AP(krows.ap().tensor, c * KROW, [[SQ, SQ], [8 * KROW, SQ], [1, SQ]])
                sp.dma_start(dst, ksb[c * SQ:(c + 1) * SQ, :, c * SQ:(c + 1) * SQ]).then_inc(s_kd, 16)
            sp.wait_ge(s_kz, 16)
            sp.wait_ge(s_kd, 16 * 8)
            for j in range(2):
                load_t(0, j)

            def slot(g, j):
                h = chan(g, j)
                if exists(g, j, 3):
                    if exists(g, j, -3):
                        sp.wait_ge(s_out[(j + 3) % SLOTS], 32 * on(g, j, 3)[0])
                    load_x(*on(g, j, 3))
                if exists(g, j, 2):
                    sp.wait_ge(s_intra, h + 1)
                    load_t(*on(g, j, 2))
                if exists(g, j, -1):
                    sp.wait_ge(s_pred, 2 * h)
                    store(*on(g, j, -1))

            groups(sp, slot)
            sp.wait_ge(s_pred, 2 * H)
            store((H - 1) // SLOTS, (H - 1) % SLOTS)
            for j in range(SLOTS):
                sp.wait_ge(s_out[j], 32 * len(range(j, H, SLOTS)))

        @block.gpsimd
        def _(pool):
            done = [0]

            def link(ins):
                done[0] += 1
                ins.then_inc(s_gp, 1)
                pool.wait_ge(s_gp, done[0])

            link(pool.memset(zpad[:], 0.0))
            link(pool.memset(ident[:], 0.0))
            link(pool.affine_select(out=ident[:], in_=ident[:], compare_op=ALU.not_equal, fill=1.0, base=0,
                                    pattern=[[-1, P]], channel_multiplier=1))
            link(pool.tensor_tensor(dmask[:], ident[:, 0:N], ident[:, N:2 * N], ALU.add))
            link(pool.iota(mask[0:B, :], pattern=[[2 * CHUNK, CPH], [1, CHUNK]], base=0, channel_multiplier=0))
            link(pool.iota(mask[B:P, :], pattern=[[2 * CHUNK, CPH], [1, CHUNK]], base=CHUNK, channel_multiplier=0))
            pool.memset(B1[:, 0, :, SQ - 1:SQ], 1.0)
            pool.memset(B2[:, 0, :, SQ - 1:SQ], 0.0).then_inc(s_pool0, 1)
            pool.wait_ge(s_pool0, 1)

            pool.wait_ge(s_spec, 2)
            double(pool, link, B1, B2, 0, 0, q3, q4)
            pool.drain().then_inc(s_btab, 1)
            pool.wait_ge(s_xini, 1)
            double(pool, link, W1, W2, 0, 4, q3, q4, 0, XSPLIT)
            pool.wait_ge(s_rhi, 3)
            for q in range(3):
                link(pool.tensor_tensor(rvl[:, q, 1], spec[:, S_R + 2 * q:S_R + 2 * q + 2, :], rvl[:, q, 0],
                                        ALU.subtract))
            pool.wait_ge(s_tabs, 1)

            def channel(g, j):
                h, k = chan(g, j), j % 2
                if exists(g, j, -2):
                    pool.wait_ge(s_et, h - 1)
                    pool.wait_ge(s_flo, h - 1)
                w1 = W1[:, :, h].unsqueeze(3).broadcast_to([P, 2, SQ, SQ])
                w2 = W2[:, :, h].unsqueeze(3).broadcast_to([P, 2, SQ, SQ])
                b1 = B1[:, 0, h].unsqueeze(1).unsqueeze(1).broadcast_to([P, 2, SQ, SQ])
                b2 = B2[:, 0, h].unsqueeze(1).unsqueeze(1).broadcast_to([P, 2, SQ, SQ])
                if exists(g, j, -1):
                    pool.wait_ge(s_pf, h)
                pool.tensor_tensor(tw1[:], w1, b1, ALU.mult).then_inc(s_gpa, 1)
                pool.tensor_tensor(tw2[:], w2, b2, ALU.mult).then_inc(s_gpa, 1)
                pool.wait_ge(s_gpa, 2 * h + 2)
                pool.tensor_tensor(pf[k][:], tw1[:].rearrange("p a b c -> p a (b c)"),
                                   tw2[:].rearrange("p a b c -> p a (b c)"), ALU.subtract).then_inc(s_pf, 1)
                if exists(g, j, -2):
                    pool.wait_ge(s_l, 3 * h - 3)
                pool.tensor_tensor(rot[k][:], dmask[:].unsqueeze(1).broadcast_to([P, 12, N]),
                                   RV[:, h].unsqueeze(2).broadcast_to([P, 12, N]), ALU.mult).then_inc(s_r, 1)

            groups(pool, channel)

        @block.scalar
        def _(act):
            def copy(dst, src):
                return act.activation(dst, src, ACT.Copy)

            def x_high(g, j, par):
                act.wait_ge(s_tr, 2 * chan(g, j) + 1 + par)
                copy(uhi[j % 2][par][:], xt[par][:]).then_inc(s_uhi[par], 1)

            act.wait_ge(s_ang, 1)
            flat = ang.rearrange("p k n -> p (k n)")
            act.activation(sn.rearrange("p k n -> p (k n)"), flat, ACT.Sin)
            act.activation(sh.rearrange("p k n -> p (k n)"), flat, ACT.Sin, scale=0.5).then_inc(s_sin, 1)
            act.wait_ge(s_lam, 1)
            for part in (slice(0, N), slice(N, 2 * N)):
                copy(nat[:, 0:16:2, part], lre[:, 0:8, :])
                ins = copy(nat[:, 1:16:2, part], lim[:, 0:8, :])
            ins.then_inc(s_nata, 1)
            for q in range((NSPEC + 3) // 4):
                n = min(4, NSPEC - 4 * q)
                act.wait_ge(s_turn, q + 1)
                copy(spec[:, 4 * q:4 * q + n, :].rearrange("p a h -> p (a h)"), pro[q][:, 0:n * P]).then_inc(s_spec, 1)
            act.wait_ge(s_spec, 7)
            for q in range(3):
                copy(rvl[:, q, 0].bitcast(F32R), spec[:, S_R + 2 * q:S_R + 2 * q + 2, :]).then_inc(s_rhi, 1)
            x_high(0, 0, 0)
            x_high(0, 0, 1)
            act.wait_ge(s_btab, 1)
            copy(bsel[0:N], B1[0:N, 0]).then_inc(s_bsel, 1)
            copy(bsel[N:P], B2[N:P, 0]).then_inc(s_bsel, 1)
            for q in range(4):
                act.wait_ge(s_k, q + 1)
                copy(ksb[:, 4 * q:4 * q + 4, :].rearrange("p a h -> p (a h)"), kbank[q][:]).then_inc(s_ksb, 1)

            def x_odd(g, j):
                act.wait_ge(s_ulo[1], chan(g, j) + 1)
                copy(uod[j % 2][:], xt[1][:]).then_inc(s_uod, 1)

            def e_high(g, j):
                act.wait_ge(s_et, chan(g, j) + 1)
                copy(ehi[j % 2][:], e_bank(j)).then_inc(s_ehi, 1)

            def f_high(g, j):
                act.wait_ge(s_pf, chan(g, j) + 1)
                if exists(g, j, -2):
                    act.wait_ge(s_y, 2 * chan(g, j) - 2)
                copy(fhi[j % 2][:], pf[j % 2][:, 1, ::-1]).then_inc(s_fhi, 1)

            def t_high(g, j):
                act.wait_ge(s_t[j % 2], 16 * (chan(g, 0) // 2 + j // 2 + 1))
                copy(thi[j % 2][:], traw[j % 2][:, ::-1]).then_inc(s_thi, 1)

            def z_high(g, j, level):
                h = chan(g, j)
                if level:
                    act.wait_ge(s_l, 3 * h + level)
                else:
                    act.wait_ge(s_in, h + 1)
                a, b = (B * c for c in ZCOLS[level])
                copy(zhi[j % 2][:, a:b], vb[j % 2][:, a:b]).then_inc(s_zhi, 1)

            def slot(g, j):
                one, two = on(g, j, 1), on(g, j, 2)
                has1, has2 = exists(g, j, 1), exists(g, j, 2)
                if has1:
                    f_high(*one)
                    x_odd(*one)
                    z_high(*one, 0)
                    t_high(*one)
                    z_high(*one, 1)
                if has2:
                    e_high(*two)
                if has1:
                    z_high(*one, 2)
                if has2:
                    x_high(*two, 0)
                    x_high(*two, 1)
                if has1:
                    z_high(*one, 3)

            e_high(0, 0)
            slot(-1, SLOTS - 1)
            groups(act, slot)

        @block.vector
        def _(dve):
            done = [0]

            def link(ins):
                done[0] += 1
                ins.then_inc(s_dve, 1)
                dve.wait_ge(s_dve, done[0])

            def less(dst, src, high):
                return dve.tensor_tensor(dst, src, high.bitcast(F32), ALU.subtract)

            def x_low(g, j, par):
                dve.wait_ge(s_uhi[par], chan(g, j) + 1)
                less(ulo[j % 2][par][:], xt[par][:], uhi[j % 2][par][:]).then_inc(s_ulo[par], 1)

            LOG2E = 1.0 / math.log(2.0)
            LN2A = 0.693359375
            LN2B = math.log(2.0) - LN2A
            ROUND = 1.5 * 2.0 ** 23

            def exp(dst, src, n, minus1=None):
                k, r, q, i = ta[:, 0:n], tb[:, 0:n], tc_[:, 0:n], ti[:, 0:n]
                link(dve.tensor_scalar(r, src, -87.0, 87.0, ALU.max, ALU.min))
                link(dve.tensor_scalar(k, r, LOG2E, ROUND, ALU.mult, ALU.add))
                link(dve.tensor_scalar(k, k, ROUND, None, ALU.subtract))
                link(dve.scalar_tensor_tensor(out=r, in0=k, scalar=-LN2A, in1=r, op0=ALU.mult, op1=ALU.add))
                link(dve.scalar_tensor_tensor(out=r, in0=k, scalar=-LN2B, in1=r, op0=ALU.mult, op1=ALU.add))
                dve.tensor_scalar(i, k, 127.0, float(2 ** 23), ALU.add, ALU.mult)
                link(dve.tensor_scalar(q, r, 1.0 / math.factorial(7), None, ALU.mult))
                for d in range(6, 0, -1):
                    link(dve.scalar_tensor_tensor(out=q, in0=q, scalar=1.0 / math.factorial(d), in1=r,
                                                  op0=ALU.add, op1=ALU.mult))
                two_k = i.bitcast(F32)
                link(dve.scalar_tensor_tensor(out=dst, in0=q, scalar=1.0, in1=two_k, op0=ALU.add, op1=ALU.mult))
                if minus1 is not None:
                    m = minus1.shape[1]
                    link(dve.tensor_tensor(q[:, 0:m], q[:, 0:m], two_k[:, 0:m], ALU.mult))
                    link(dve.scalar_tensor_tensor(out=minus1, in0=two_k[:, 0:m], scalar=-1.0, in1=q[:, 0:m],
                                                  op0=ALU.add, op1=ALU.add))

            dve.wait_ge(s_prm, 16 * 4)
            exp(ex0[:], prm[:], 1 + N)
            dt = ex0[:, 0:1]
            link(dve.tensor_scalar(arg[:, 0, :], ex0[:, 1:1 + N], dt, -1.0, ALU.mult, ALU.mult))
            link(dve.tensor_scalar(ang[:, 0, :], aim[:], dt, None, ALU.mult))
            for k in range(1, 6):
                dve.tensor_scalar(arg[:, k, :], arg[:, 0, :], float(POWERS[2 * k]), None, ALU.mult)
            for k in range(1, NPOW):
                ins = dve.tensor_scalar(ang[:, k, :], ang[:, 0, :], float(POWERS[k]), None, ALU.mult)
            link(ins)
            c1 = 6.28125
            c2 = round((2 * math.pi - c1) * 2 ** 21) / 2 ** 21
            c3 = 2 * math.pi - c1 - c2
            flat = ang.rearrange("p k n -> p (k n)")
            link(dve.tensor_scalar(ta, flat, 1.0 / (2 * math.pi), ROUND, ALU.mult, ALU.add))
            link(dve.tensor_scalar(ta, ta, ROUND, None, ALU.subtract))
            for c in (c1, c2, c3):
                link(dve.scalar_tensor_tensor(out=flat, in0=ta, scalar=-c, in1=flat, op0=ALU.mult, op1=ALU.add))
            link(dve.tensor_scalar(flat, flat, 3.1415925, -3.1415925, ALU.min, ALU.max))
            dve.tensor_copy(cs[:, 0, 0:1], ex0[:, 0:1]).then_inc(s_ang, 1)
            exp(mexp, arg[:, 0:6, :].rearrange("p k n -> p (k n)"), 6 * N, em1[:])
            dve.tensor_copy(mag[:, 0:NPOW:2, :], mexp.rearrange("p (k n) -> p k n", n=N))
            link(dve.tensor_tensor(mag[:, 1:NPOW:2, :], mexp[:, 0:5 * N].rearrange("p (k n) -> p k n", n=N),
                                   mexp[:, 0:5 * N].rearrange("p (k n) -> p k n", n=N), ALU.mult))
            dve.wait_ge(s_sin, 1)
            m, s, f = (t.rearrange("p k n -> p (k n)") for t in (mag, sh, sn))
            link(dve.scalar_tensor_tensor(out=ta, in0=s, scalar=-2.0, in1=s, op0=ALU.mult, op1=ALU.mult))
            dve.tensor_tensor(lim.rearrange("p k n -> p (k n)"), m, f, ALU.mult)
            link(dve.tensor_tensor(ta, m, ta, ALU.mult))
            dve.tensor_tensor(lre.rearrange("p k n -> p (k n)"), m, ta, ALU.add).then_inc(s_lam, 1)
            dve.wait_ge(s_lam, 1)
            l1r, l1i, n1, n2, dn, t1, cr, ci = (cs[:, i, :] for i in range(8))
            ar, ai = ex0[:, 1:1 + N], aim[:]
            link(dve.tensor_tensor(l1r, em1[:], ta[:, 0:N], ALU.add))
            l1i = lim[:, 0, :]
            dve.tensor_tensor(dn, ar, ar, ALU.mult)
            link(dve.tensor_tensor(t1, ai, ai, ALU.mult))
            link(dve.tensor_tensor(dn, dn, t1, ALU.add))
            link(dve.reciprocal(dn, dn))
            dve.tensor_tensor(n1, l1i, ai, ALU.mult)
            link(dve.tensor_tensor(t1, l1r, ar, ALU.mult))
            link(dve.tensor_tensor(n1, n1, t1, ALU.subtract))
            dve.tensor_tensor(n2, l1r, ai, ALU.mult)
            link(dve.tensor_tensor(t1, l1i, ar, ALU.mult))
            link(dve.scalar_tensor_tensor(out=n2, in0=n2, scalar=-1.0, in1=t1, op0=ALU.mult, op1=ALU.subtract))
            link(dve.tensor_tensor(n1, n1, dn, ALU.mult))
            link(dve.tensor_tensor(n2, n2, dn, ALU.mult))
            c_re = cin[:].rearrange("p (n c) -> p c n", c=2)[:, 0, :]
            c_im = cin[:].rearrange("p (n c) -> p c n", c=2)[:, 1, :]
            dve.tensor_tensor(cr, c_re, n1, ALU.mult)
            link(dve.tensor_tensor(t1, c_im, n2, ALU.mult))
            link(dve.tensor_tensor(cr, cr, t1, ALU.subtract))
            dve.tensor_tensor(ci, c_re, n2, ALU.mult)
            link(dve.tensor_tensor(t1, c_im, n1, ALU.mult))
            link(dve.tensor_tensor(ci, ci, t1, ALU.add))
            re, im = slice(0, N), slice(N, 2 * N)

            def put(row, part, src, factor=1.0):
                return dve.tensor_scalar(nat[:, row, part], src, factor, None, ALU.mult)

            put(S_X1, re, lre[:, 0, :])
            put(S_X1, im, lim[:, 0, :])
            put(S_X2, re, lim[:, 0, :])
            put(S_X2, im, lre[:, 0, :], -1.0)
            put(S_Y1, re, cr, 2.0)
            put(S_Y1, im, ci, -2.0)
            put(S_Y2, re, ci, 2.0)
            put(S_Y2, im, cr, 2.0)
            for q in range(3):
                put(S_R + 2 * q, re, lre[:, 8 + q, :])
                put(S_R + 2 * q, im, lim[:, 8 + q, :], -1.0)
                put(S_R + 2 * q + 1, re, lim[:, 8 + q, :])
                ins = put(S_R + 2 * q + 1, im, lre[:, 8 + q, :])
            ins.then_inc(s_nat, 1)
            dve.wait_ge(s_spec, 5)
            dve.tensor_copy(W1[:, 1, :, SQ - 1], spec[:, S_Y1, :])
            dve.tensor_copy(W2[:, 1, :, SQ - 1], spec[:, S_Y2, :])
            dve.tensor_copy(W1[:, 0, :, SQ - 1], spec[:, S_X1, :])
            dve.tensor_copy(W2[:, 0, :, SQ - 1], spec[:, S_X2, :]).then_inc(s_xini, 1)
            dve.wait_ge(s_xini, 1)
            double(dve, link, W1, W2, 1, 4, q1, q2)
            dve.engine_nop().then_inc(s_ytab, 1)
            x_low(0, 0, 0)
            x_low(0, 0, 1)
            for k in range(2):
                dve.memset(zhi[k][:, 0:B].bitcast(F32), 0.0)
                dve.memset(zlo[k][:, 0:B].bitcast(F32), 0.0)
            double(dve, link, W1, W2, 0, 4, q1, q2, XSPLIT, H)
            dve.engine_nop().then_inc(s_tabs, 1)
            dve.wait_ge(s_len, 48)
            dve.wait_ge(s_pool0, 1)
            dve.tensor_copy(flen[:], ilen[:])
            link(dve.tensor_reduce(dsel[:], ident[:, SQ - 1:P:SQ], mybir.AxisListType.X, ALU.add))
            link(dve.tensor_scalar(dall[:], dall[:], 1.0, dsel[:, 0:1], ALU.add, ALU.mult))
            k0 = ksb.rearrange("p g (c i) -> p g c i", i=SQ)[:, :, :, SQ - 1]
            dve.wait_ge(s_ksb, 4)
            dve.tensor_tensor(k0, k0, dall[:].rearrange("p (g c) -> p g c", c=8), ALU.add).then_inc(s_kfin, 1)
            link(dve.tensor_scalar(mask[:], mask[:], flen[:, 0:1], None, ALU.is_lt))

            def e_low(g, j):
                dve.wait_ge(s_ehi, chan(g, j) + 1)
                less(elo[j % 2][:], e_bank(j), ehi[j % 2][:]).then_inc(s_elo, 1)

            def f_low(g, j):
                dve.wait_ge(s_fhi, chan(g, j) + 1)
                less(flo[j % 2][:], pf[j % 2][:, 1, ::-1], fhi[j % 2][:]).then_inc(s_flo, 1)

            def t_low(g, j):
                dve.wait_ge(s_thi, chan(g, j) + 1)
                less(tlo[j % 2][:], traw[j % 2][:, ::-1], thi[j % 2][:]).then_inc(s_tlo, 1)

            def z_low(g, j, level):
                a, b = (B * c for c in ZCOLS[level])
                dve.wait_ge(s_zhi, 4 * chan(g, j) + level + 1)
                less(zlo[j % 2][:, a:b], vb[j % 2][:, a:b], zhi[j % 2][:, a:b]).then_inc(s_zlo, 1)

            def choose(g, j, part):
                a = part * 512
                dve.copy_predicated(xs[j][:, a:a + 512], mask[:, a:a + 512], yb[j % 2][part][:]).then_inc(s_pred, 1)

            def slot(g, j):
                h = chan(g, j)
                one, two, back = on(g, j, 1), on(g, j, 2), on(g, j, -1)
                has1, has2, hasb = exists(g, j, 1), exists(g, j, 2), exists(g, j, -1)
                if hasb:
                    dve.wait_ge(s_y, 2 * h)
                if has1:
                    f_low(*one)
                if hasb:
                    choose(*back, 0)
                if has1:
                    z_low(*one, 0)
                if hasb:
                    choose(*back, 1)
                if has1:
                    t_low(*one)
                    z_low(*one, 1)
                if has2:
                    e_low(*two)
                if has1:
                    z_low(*one, 2)
                if has2:
                    x_low(*two, 0)
                    x_low(*two, 1)
                if has1:
                    z_low(*one, 3)

            e_low(0, 0)
            slot(-1, SLOTS - 1)
            groups(dve, slot)
            for part in range(2):
                dve.wait_ge(s_y, 2 * H - 1 + part)
                choose((H - 1) // SLOTS, (H - 1) % SLOTS, part)

        @block.tensor
        def _(pe):
            pe.wait_ge(s_pool0, 1)
            pe.wait_ge(s_nata, 1)
            for q in range((NSPEC + 3) // 4):
                n = min(4, NSPEC - 4 * q)
                if q == 4:
                    pe.wait_ge(s_nat, 1)
                for r in range(n):
                    mm = pe.transpose(pro[q][:, r * P:(r + 1) * P], nat[:, 4 * q + r, :], ident[:])
                mm.then_inc(s_turn, 1)
            def turn_x(g, j, par):
                pe.wait_ge(s_x[j], 32 * (g + 1))
                for c in range(CPH):
                    b = 2 * c + par
                    mm = pe.transpose(xt[par][:, c * P:(c + 1) * P], xs[j][:, b * BLK:(b + 1) * BLK], ident[:])
                mm.then_inc(s_tr, 1)

            def turn_e(g, j):
                pe.wait_ge(s_pf, chan(g, j) + 1)
                if exists(g, j, -3):
                    pe.wait_ge(s_pred, 2 * chan(g, j) - 4)
                pe.transpose(e_bank(j)[:, 0:P], pf[j % 2][:, 0, 0:P], ident[:])
                pe.transpose(e_bank(j)[:, P:2 * P], pf[j % 2][:, 0, P:2 * P], ident[:]).then_inc(s_et, 1)

            def three(o, a_hi, a_lo, b_hi, b_lo, start, stop):
                pe.matmul(o, a_hi, b_hi, start=start, stop=False, skip_group_check=True)
                pe.matmul(o, a_hi, b_lo, start=False, stop=False, skip_group_check=True)
                return pe.matmul(o, a_lo, b_hi, start=False, stop=stop, skip_group_check=True)

            def chunk_sums(g, j):
                h, k = chan(g, j), j % 2
                cols = slice(0, (NC - 1) * B)
                pe.wait_ge(s_elo, h + 1)
                if exists(g, j, -2):
                    pe.wait_ge(s_zlo, 4 * h - 4)
                for par in range(2):
                    pe.wait_ge(s_ulo[par], h + 1)
                    e = slice(par * P, (par + 1) * P)
                    mm = three(vb[k][:, B:NC * B], ehi[k][:, e], elo[k][:, e], uhi[k][par][:, cols],
                               ulo[k][par][:, cols], par == 0, False)
                mm.then_inc(s_in, 1)

            def hop(g, j, level):
                h, k = chan(g, j), j % 2
                if level == 0:
                    pe.wait_ge(s_r, h + 1)
                pe.wait_ge(s_zlo, 4 * h + level + 1)
                a, b, by = HOPS[level]
                w = [rot[k][:, 4 * level + 2 * i:4 * level + 2 * i + 2, :].rearrange("p c n -> p (c n)")
                     for i in range(2)]
                cols = slice(B * a, B * b)
                three(vb[k][:, B * (a + by):B * (b + by)], w[0], w[1], zhi[k][:, cols], zlo[k][:, cols], False,
                      level == 2).then_inc(s_l, 1)

            def y_cols(g, j, c):
                return yb[j % 2][c // 2][:, (c % 2) * CHUNK:(c % 2 + 1) * CHUNK]

            def toep_even(g, j, c):
                k, b = j % 2, slice(c * P, (c + 1) * P)
                if c == 0:
                    pe.wait_ge(s_tlo, chan(g, j) + 1)
                    if exists(g, j, -2):
                        pe.wait_ge(s_pred, 2 * chan(g, j) - 2)
                three(y_cols(g, j, c), uhi[k][0][:, b], ulo[k][0][:, b], thi[k][:], tlo[k][:], c % 2 == 0, False)

            def toep_odd(g, j, c):
                k, b = j % 2, slice(c * P, (c + 1) * P)
                if c == 0:
                    pe.wait_ge(s_uod, chan(g, j) + 1)
                mm = pe.matmul(y_cols(g, j, c)[:, BLK:2 * BLK], uod[k][:, b], traw[k][:, :BLK - 1:-1], start=False,
                               stop=False, skip_group_check=True)
                if c == CPH - 1:
                    mm.then_inc(s_intra, 1)

            def from_state(g, j, c):
                k, b = j % 2, slice(c * P, (c + 1) * P)
                if c == 0:
                    pe.wait_ge(s_flo, chan(g, j) + 1)
                    pe.wait_ge(s_zlo, 4 * chan(g, j) + 4)
                mm = three(y_cols(g, j, c), zhi[k][:, b], zlo[k][:, b], fhi[k][:], flo[k][:], False, c % 2 == 1)
                if c % 2:
                    mm.then_inc(s_y, 1)

            def slot(g, j):
                here, one, two = (g, j), on(g, j, 1), on(g, j, 2)
                has0, has1, has2 = exists(g, j, 0), exists(g, j, 1), exists(g, j, 2)
                if has1:
                    chunk_sums(*one)
                if has0:
                    toep_even(*here, 0)
                    toep_odd(*here, 0)
                    toep_even(*here, 1)
                    toep_odd(*here, 1)
                    toep_even(*here, 2)
                if has1:
                    hop(*one, 0)
                if has0:
                    toep_odd(*here, 2)
                    toep_even(*here, 3)
                    toep_odd(*here, 3)
                if has2:
                    turn_e(*two)
                    turn_x(*two, 0)
                if has1:
                    hop(*one, 1)
                if has2:
                    turn_x(*two, 1)
                if has0:
                    from_state(*here, 0)
                    from_state(*here, 1)
                if has1:
                    hop(*one, 2)
                if has0:
                    from_state(*here, 2)
                    from_state(*here, 3)

            pe.wait_ge(s_spec, 7)
            turn_x(0, 0, 0)
            turn_x(0, 0, 1)
            pe.wait_ge(s_bsel, 2)
            pe.wait_ge(s_ytab, 1)
            for g in range(H // 8):
                mm = pe.matmul(kbank[g // 4][:, (g % 4) * P:(g % 4 + 1) * P],
                               W1[:, 1, 8 * g:8 * g + 8, :].rearrange("p c i -> p (c i)"),
                               bsel[:, 8 * g:8 * g + 8, :].rearrange("p c i -> p (c i)"), start=True, stop=True)
                if g % 4 == 3:
                    mm.then_inc(s_k, 1)
            turn_e(0, 0)
            pe.wait_ge(s_ksb, 4)
            slot(-1, SLOTS - 1)
            groups(pe, slot)


_INS = ['x', 'itok_B_8_3872', 'L0_cond_log_dt', 'L0_cond_C', 'L0_cond_log_A_real', 'L0_cond_A_imag', 'L0_cond_D']


def kernel(**inputs):
    import numpy as _np
    import concourse.bacc as _bacc
    from concourse import mybir as _mybir
    from concourse.bass_utils import run_bass_kernel_spmd as _run

    nc = _bacc.Bacc("TRN2", target_bir_lowering=False, num_devices=1)
    arrays, args = {}, []
    for name in _INS:
        a = _np.ascontiguousarray(inputs[name])
        arrays[f"in_{name}_dram"] = a
        args.append(nc.dram_tensor(f"in_{name}_dram", a.shape, _mybir.dt.from_np(a.dtype), kind="ExternalInput").ap())
    out = nc.dram_tensor("out_0_dram", inputs["x"].shape, _mybir.dt.float32, kind="ExternalOutput").ap()
    s4d_kernel(nc, *args, out)
    r = _run(nc, [arrays], core_ids=[0])
    return r.results[0]["out_0_dram"]
```

```python
import math
from contextlib import ExitStack

import concourse.bass as bass
from concourse import mybir

ALU = mybir.AluOpType
ACT = mybir.ActivationFunctionType
F32 = mybir.dt.float32
F32R = mybir.dt.float32r
I32 = mybir.dt.int32

B, H, L, N = 64, 128, 2048, 64
P = 128
BLK = 128
CHUNK = 2 * BLK
HALF = L // 2
CPH = HALF // CHUNK
NC = 2 * CPH
SQ = 16
SLOTS = 6
GROUPS = H // SLOTS
KROW = 384
PAD = BLK - 1
POWERS = [2 ** k for k in range(11)]
NPOW = len(POWERS)
R_POW = POWERS.index(CHUNK)
A_POW = POWERS.index(SQ)
ZCOLS = [(1, 7), (2, 6), (3, 5), (5, 8)]
HOPS = [(1, 7, 1), (1, 6, 2), (0, 4, 4)]

XSPLIT = 40
BANKS = 6
STEPS = [("Y1", 8), ("Y1", 12), ("bsel", 8), ("bsel", 12), ("Y1", 0), ("Y1", 4),
         ("B1", 8), ("B1", 12), ("B2", 8), ("B2", 12), ("Y2", 0), ("Y2", 4), ("Y2", 8), ("Y2", 12),
         ("bsel", 0), ("bsel", 4), ("X1", 8), ("X2", 8), ("X1", 12), ("X2", 12),
         ("B1", 0), ("B1", 4), ("B2", 0), ("B2", 4), ("K", 0), ("K", 4), ("K", 8), ("K", 12),
         ("X1", 0), ("X2", 0), ("X1", 4), ("X2", 4), ("R", 0), ("R", 4), ("R", 8)]
T_BSEL = STEPS.index(("bsel", 4))
T_K = STEPS.index(("K", 0))
T_R = STEPS.index(("R", 0))
T_END = len(STEPS)
WARM_TABLES, WARM_LOOP, WARM_SCAN = 32, 18, 10
BY_VECTOR = [20, 21, 23, 26, 29, 31, 33]


def s4d_kernel(nc, x, length, log_dt, C, log_A_real, A_imag, D, out):
    ctx = ExitStack()
    with ctx:
        def sb(name, shape, dt=F32):
            return ctx.enter_context(nc.sbuf_tensor(name, shape, dt))

        def sem(name):
            return ctx.enter_context(nc.semaphore(name))

        krows = nc.dram_tensor("krows", [H, KROW], F32)

        prm = sb("prm", [P, 1 + N])
        cin = sb("cin", [P, 2 * N])
        aim = sb("aim", [P, N])
        dall = sb("dall", [P, H])
        dsel = sb("dsel", [P, 1])
        ilen = sb("ilen", [P, 1], I32)
        flen = sb("flen", [P, 1])
        ex0 = sb("ex0", [P, 1 + N])
        wide = sb("wide", [P, 3 * NPOW * N])
        em1 = sb("em1", [P, N])
        small = sb("small", [P, 7, N])
        lre_flat = sb("lre", [P, NPOW * N])
        NY = sb("NY", [P, SQ, 3, N])
        NR = sb("NR", [P, 3, 2, 3, N])
        ksb = sb("ksb", [P, SQ, P])
        ident = sb("ident", [P, P])
        dmask = sb("dmask", [P, N])
        W1 = sb("W1", [P, 2, H, SQ])
        W2 = sb("W2", [P, 2, H, SQ])
        B1 = sb("B1", [P, H, SQ])
        B2 = sb("B2", [P, H, SQ])
        q1 = sb("q1", [P, NPOW * N])
        q2 = sb("q2", [P, NPOW * N])
        q3 = sb("q3", [P, NPOW * N])
        q4 = sb("q4", [P, NPOW * N])
        RV = sb("RV", [P, H, 12])
        bsel = sb("bsel", [P, H, SQ])
        zpad = sb("zpad", [P, PAD])
        mask = sb("mask", [P, HALF], I32)
        xall = sb("xall", [P, SLOTS, HALF])
        xs = [xall[:, i, :] for i in range(SLOTS)]
        room = sb("room", [P, 8, NC * B])
        uhi = [[sb(f"uhi{i}{p}", [P, NC * B], F32R) for p in range(2)] for i in range(2)]
        ulo = [[sb(f"ulo{i}{p}", [P, NC * B], F32R) for p in range(2)] for i in range(2)]
        uod = [sb("uod0", [P, NC * B]), room[:, 4]]
        zhi = [sb(f"zhi{i}", [P, NC * B], F32R) for i in range(2)]
        zlo = [sb(f"zlo{i}", [P, NC * B], F32R) for i in range(2)]
        ehi = [sb(f"ehi{i}", [P, 2 * P], F32R) for i in range(2)]
        elo = [sb(f"elo{i}", [P, 2 * P], F32R) for i in range(2)]
        rot = [sb(f"rot{i}", [P, 12, N], F32R) for i in range(2)]
        tw1, tw2 = (room[:, i].rearrange("p (a b c) -> p a b c", a=2, b=SQ) for i in (5, 6))
        pf = [sb("pf0", [P, 2, CHUNK]), room[:, 7].rearrange("p (a q) -> p a q", a=2)]
        fhi = [sb(f"fhi{i}", [P, CHUNK], F32R) for i in range(2)]
        flo = [sb(f"flo{i}", [P, CHUNK], F32R) for i in range(2)]
        traw = [sb(f"traw{i}", [P, CHUNK]) for i in range(2)]
        thi = [sb(f"thi{i}", [P, CHUNK], F32R) for i in range(2)]
        tlo = [sb(f"tlo{i}", [P, CHUNK], F32R) for i in range(2)]

        npn = NPOW * N

        def view(t, a=0):
            return t[:, a:a + npn].rearrange("p (k n) -> p k n", n=N)
        arg = view(q4)
        lre = view(lre_flat[:])
        NB = room[:].rearrange("p s t -> p (s t)").rearrange("p (i c n) -> p i c n", i=SQ, n=N)
        NX = xall[:, 3:SLOTS, :].rearrange("p s t -> p (s t)").rearrange("p (i c n) -> p i c n", i=SQ, n=N)
        w2_flat = W2[:].rearrange("p a h i -> p (a h i)")
        mag, sn, sh = (view(w2_flat, q * npn) for q in range(3))
        ang, lim = view(wide), view(wide, npn)
        whole = wide[:, 2 * npn:3 * npn]

        def bank(name):
            return ctx.enter_context(nc.psum_tensor(name, [P, 512], F32))
        xt = [bank("xt_even"), bank("xt_odd")]
        vb = [bank(f"v{i}") for i in range(2)]
        yb = [[bank(f"y{i}{k}") for k in range(2)] for i in range(2)]
        pro = [vb[0], vb[1], yb[0][0], yb[0][1], yb[1][0], yb[1][1]]

        l1r, norm, g_re, g_im, t1, t2, t3 = (small[:, i, :] for i in range(7))
        ar, ai = ex0[:, 1:1 + N], aim[:]

        s_prm = sem("s_prm")
        s_ca = sem("s_ca")
        s_len = sem("s_len")
        s_pool0 = sem("s_pool0")
        s_dve = sem("s_dve")
        s_gp = sem("s_gp")
        s_arg = sem("s_arg")
        s_ang = sem("s_ang")
        s_sin = sem("s_sin")
        s_lam = sem("s_lam")
        s_ex0 = sem("s_ex0")
        s_norm = sem("s_norm")
        s_g = sem("s_g")
        s_nb = sem("s_nb")
        s_ny = sem("s_ny")
        s_nx = sem("s_nx")
        s_nxp = sem("s_nxp")
        s_yneg = sem("s_yneg")
        s_xneg = sem("s_xneg")
        s_bdup = sem("s_bdup")
        s_rlo = sem("s_rlo")
        s_fill = [sem(f"s_fill{b}") for b in range(BANKS)]
        s_free = [sem(f"s_free{b}") for b in range(BANKS)]
        s_rhi = sem("s_rhi")
        s_kfin = sem("s_kfin")
        s_xini = sem("s_xini")
        s_gpa = sem("s_gpa")
        s_kz = sem("s_kz")
        s_kd = sem("s_kd")
        s_x = [sem(f"s_x{i}") for i in range(SLOTS)]
        s_out = [sem(f"s_out{i}") for i in range(SLOTS)]
        s_t = [sem(f"s_t{i}") for i in range(2)]
        s_tr = sem("s_tr")
        s_et = sem("s_et")
        s_in = sem("s_in")
        s_l = sem("s_l")
        s_intra = sem("s_intra")
        s_y = sem("s_y")
        s_uhi = [sem(f"s_uhi{p}") for p in range(2)]
        s_ulo = [sem(f"s_ulo{p}") for p in range(2)]
        s_uod = sem("s_uod")
        s_zhi = sem("s_zhi")
        s_zlo = sem("s_zlo")
        s_ehi = sem("s_ehi")
        s_elo = sem("s_elo")
        s_fhi = sem("s_fhi")
        s_flo = sem("s_flo")
        s_thi = sem("s_thi")
        s_tlo = sem("s_tlo")
        s_pred = sem("s_pred")
        s_pf = sem("s_pf")
        s_r = sem("s_r")

        x_v = x.rearrange("b h (m f t) -> h f b m t", f=2, t=CHUNK)
        o_v = out.rearrange("b h (m f t) -> h f b m t", f=2, t=CHUNK)

        def groups(eng, body):
            for j in range(SLOTS):
                body(0, j)
            with eng.Fori(1, GROUPS - 1) as g:
                for j in range(SLOTS):
                    body(g, j)
            for h in range((GROUPS - 1) * SLOTS, H):
                body(h // SLOTS, h % SLOTS)

        def e_bank(j):
            return yb[(j + 1) % 2][1][:, 0:2 * P]

        def on(g, j, d):
            return g + (j + d) // SLOTS, (j + d) % SLOTS

        def chan(g, j):
            return g * SLOTS + j

        def exists(g, j, d):
            return not isinstance(g, int) or 0 <= chan(g, j) + d < H

        def half(n):
            return slice(SQ // 2, SQ) if n == 0 else slice(0, SQ // 2)

        def level(eng, link, table, re, im, first, temps, k, lo=0, hi=N):
            m = 2 ** k
            old, new = slice(SQ - m, SQ), slice(SQ - 2 * m, SQ - m)
            c, s = (t[:, first + k, lo:hi].unsqueeze(1).broadcast_to([P, m, hi - lo]) for t in (lre, lim))
            rc, is_, rs, ic = (t[:, 0:(hi - lo) * m].rearrange("p (m n) -> p m n", m=m) for t in temps)
            eng.tensor_tensor(rc, table[:, old, re, lo:hi], c, ALU.mult)
            eng.tensor_tensor(is_, table[:, old, im, lo:hi], s, ALU.mult)
            eng.tensor_tensor(rs, table[:, old, re, lo:hi], s, ALU.mult)
            link(eng.tensor_tensor(ic, table[:, old, im, lo:hi], c, ALU.mult))
            eng.tensor_tensor(table[:, new, re, lo:hi], rc, is_, ALU.subtract)
            return eng.tensor_tensor(table[:, new, im, lo:hi], rs, ic, ALU.add)

        def minus(eng, table, n):
            return eng.tensor_scalar(table[:, half(n), 2, :], table[:, half(n), 0, :], -1.0, None, ALU.mult)

        def filled(eng, t):
            eng.wait_ge(s_fill[t % BANKS], t // BANKS + 1)

        def four(t):
            return pro[t % BANKS][:].rearrange("p (i h) -> p i h", h=H)

        def place(t):
            table, i = STEPS[t]
            if table == "K":
                return ksb[:, i:i + 4, :]
            whole = {"Y1": W1[:, 1], "Y2": W2[:, 1], "X1": W1[:, 0], "X2": W2[:, 0], "B1": B1[:], "B2": B2[:],
                     "bsel": bsel[:], "R": RV[:]}[table]
            return whole[:, :, i:i + 4].rearrange("p h i -> p i h")

        block = ctx.enter_context(nc.Block())

        @block.sync
        def _(sp):
            sp.dma_start(prm[:, 0:1], log_dt.rearrange("(h a) -> h a", a=1)).then_inc(s_prm, 16)
            sp.dma_start(prm[:, 1:1 + N], log_A_real).then_inc(s_prm, 16)
            sp.dma_start(cin[:], C.rearrange("h n c -> h (n c)")).then_inc(s_ca, 16)
            sp.dma_start(aim[:], A_imag).then_inc(s_ca, 16)
            sp.dma_start(dall[:], D.rearrange("(a h) -> a h", a=1).broadcast_to([P, H])).then_inc(s_len, 16)
            for f in range(2):
                sp.dma_start(ilen[f * B:(f + 1) * B, :], length.rearrange("(b a) -> b a", a=1)).then_inc(s_len, 16)

            def load_x(g, j):
                for f in range(2):
                    sp.dma_start(xs[j][f * B:(f + 1) * B, :].rearrange("p (m t) -> p m t", t=CHUNK),
                                 x_v[chan(g, j), f]).then_inc(s_x[j], 16)

            def store(g, j, m=slice(0, CPH)):
                for f in range(2):
                    sp.dma_start(o_v[chan(g, j), f, :, m],
                                 xs[j][f * B:(f + 1) * B, :].rearrange("p (m t) -> p m t", t=CHUNK)[:, m]
                                 ).then_inc(s_out[j], 16)

            def load_t(g, j):
                src = bass.AP(krows.ap().tensor, chan(g, j) * KROW, [[1, P], [1, CHUNK]])
                sp.dma_start(traw[j % 2][:], src).then_inc(s_t[j % 2], 16)

            for j in range(3):
                load_x(0, j)
            sp.wait_ge(s_pool0, 1)
            sp.dma_start(krows.ap()[:, CHUNK:CHUNK + PAD], zpad[:]).then_inc(s_kz, 16)
            sp.wait_ge(s_kfin, 1)
            for c in range(8):
                dst = bass.AP(krows.ap().tensor, c * KROW, [[SQ, SQ], [8 * KROW, SQ], [1, SQ]])
                sp.dma_start(dst, ksb[c * SQ:(c + 1) * SQ, :, c * SQ:(c + 1) * SQ]).then_inc(s_kd, 16)
            sp.wait_ge(s_kz, 16)
            sp.wait_ge(s_kd, 16 * 8)
            for j in range(2):
                load_t(0, j)

            def slot(g, j):
                h = chan(g, j)
                if exists(g, j, 3):
                    if exists(g, j, -3):
                        sp.wait_ge(s_out[(j + 3) % SLOTS], 32 * on(g, j, 3)[0])
                    load_x(*on(g, j, 3))
                if exists(g, j, 2):
                    sp.wait_ge(s_intra, h + 1)
                    load_t(*on(g, j, 2))
                if exists(g, j, -1):
                    sp.wait_ge(s_pred, 2 * h)
                    store(*on(g, j, -1))

            filled(sp, T_END - 1)
            groups(sp, slot)
            last = ((H - 1) // SLOTS, (H - 1) % SLOTS)
            for part in range(2):
                sp.wait_ge(s_pred, 2 * H - 1 + part)
                store(*last, slice(part * CPH // 2, (part + 1) * CPH // 2))
            for j in range(SLOTS):
                sp.wait_ge(s_out[j], 32 * len(range(j, H, SLOTS)) + (32 if j == last[1] else 0))

        @block.gpsimd
        def _(pool):
            done = [0]

            def link(ins):
                done[0] += 1
                ins.then_inc(s_gp, 1)
                pool.wait_ge(s_gp, done[0])

            link(pool.memset(zpad[:], 0.0))
            link(pool.memset(ident[:], 0.0))
            link(pool.affine_select(out=ident[:], in_=ident[:], compare_op=ALU.not_equal, fill=1.0, base=0,
                                    pattern=[[-1, P]], channel_multiplier=1))
            link(pool.tensor_tensor(dmask[:], ident[:, 0:N], ident[:, N:2 * N], ALU.add))
            link(pool.iota(mask[0:B, :], pattern=[[2 * CHUNK, CPH], [1, CHUNK]], base=0, channel_multiplier=0))
            link(pool.iota(mask[B:P, :], pattern=[[2 * CHUNK, CPH], [1, CHUNK]], base=CHUNK, channel_multiplier=0))
            pool.engine_nop().then_inc(s_pool0, 1)

            pool.wait_ge(s_ex0, 1)
            pool.wait_ge(s_ca, 16 * 2)
            c_re = cin[:].rearrange("p (n c) -> p c n", c=2)[:, 0, :]
            c_im = cin[:].rearrange("p (n c) -> p c n", c=2)[:, 1, :]
            pool.tensor_tensor(t1, ar, ar, ALU.mult)
            link(pool.tensor_tensor(t2, ai, ai, ALU.mult))
            pool.tensor_tensor(norm, t1, t2, ALU.add).then_inc(s_norm, 1)
            link(pool.tensor_tensor(t3, c_im, ai, ALU.mult))
            link(pool.tensor_tensor(g_re, c_re, ar, ALU.mult))
            link(pool.tensor_tensor(g_re, t3, g_re, ALU.subtract))
            link(pool.tensor_tensor(t3, c_im, ar, ALU.mult))
            link(pool.tensor_tensor(g_im, c_re, ai, ALU.mult))
            link(pool.tensor_tensor(g_im, g_im, t3, ALU.add))
            pool.wait_ge(s_norm, 2)
            pool.tensor_tensor(g_re, g_re, norm, ALU.mult).then_inc(s_g, 1)
            pool.tensor_tensor(g_im, g_im, norm, ALU.mult).then_inc(s_g, 1)
            pool.memset(NB[:, SQ - 1, 1, :], 1.0)
            link(pool.memset(NB[:, SQ - 1, 2, :], 0.0))
            pool.wait_ge(s_lam, 1)
            room_x = W1[:, 0].rearrange("p h i -> p (h i)")
            temps = [room_x[:, q * SQ // 2 * N:(q + 1) * SQ // 2 * N] for q in range(4)]
            link(level(pool, link, NB, 1, 2, 0, temps, 0))
            link(level(pool, link, NB, 1, 2, 0, temps, 1))
            level(pool, link, NB, 1, 2, 0, temps, 2).then_inc(s_nb, 1)
            pool.wait_ge(s_nb, 1)
            level(pool, link, NB, 1, 2, 0, temps, 3).then_inc(s_nb, 1)
            pool.wait_ge(s_nx, 1)
            part = SQ // 2 * (N - XSPLIT)
            temps = [wide[:, a:a + part] for a in (0, part, 2 * npn, 2 * npn + part)]
            level(pool, link, NX, 0, 1, A_POW, temps, 3, XSPLIT, N).then_inc(s_nxp, 1)
            for t in range(T_R - BANKS, T_R):
                pool.wait_ge(s_free[t % BANKS], t // BANKS + 1)

            def channel(g, j):
                h, k = chan(g, j), j % 2
                if exists(g, j, -2):
                    pool.wait_ge(s_et, h - 1)
                    pool.wait_ge(s_flo, h - 1)
                w1 = W1[:, :, h].unsqueeze(3).broadcast_to([P, 2, SQ, SQ])
                w2 = W2[:, :, h].unsqueeze(3).broadcast_to([P, 2, SQ, SQ])
                b1 = B1[:, h].unsqueeze(1).unsqueeze(1).broadcast_to([P, 2, SQ, SQ])
                b2 = B2[:, h].unsqueeze(1).unsqueeze(1).broadcast_to([P, 2, SQ, SQ])
                if exists(g, j, -1):
                    pool.wait_ge(s_pf, h)
                pool.tensor_tensor(tw1[:], w1, b1, ALU.mult).then_inc(s_gpa, 1)
                pool.tensor_tensor(tw2[:], w2, b2, ALU.mult).then_inc(s_gpa, 1)
                pool.wait_ge(s_gpa, 2 * h + 2)
                pool.tensor_tensor(pf[k][:], tw1[:].rearrange("p a b c -> p a (b c)"),
                                   tw2[:].rearrange("p a b c -> p a (b c)"), ALU.subtract).then_inc(s_pf, 1)
                if exists(g, j, -2):
                    pool.wait_ge(s_l, 3 * h - 3)
                if not exists(g, j, -1):
                    for t in range(T_R, T_END):
                        pool.wait_ge(s_free[t % BANKS], t // BANKS + 1)
                pool.tensor_tensor(rot[k][:], dmask[:].unsqueeze(1).broadcast_to([P, 12, N]),
                                   RV[:, h].unsqueeze(2).broadcast_to([P, 12, N]), ALU.mult).then_inc(s_r, 1)

            groups(pool, channel)

        @block.scalar
        def _(act):
            def copy(dst, src):
                return act.activation(dst, src, ACT.Copy)

            def x_high(g, j, par):
                act.wait_ge(s_tr, 2 * chan(g, j) + 1 + par)
                copy(uhi[j % 2][par][:], xt[par][:]).then_inc(s_uhi[par], 1)

            act.wait_ge(s_arg, 1)
            for k in range(1, len(POWERS[::2])):
                act.activation(arg[:, k, :], arg[:, 0, :], ACT.Copy, scale=float(POWERS[2 * k])).then_inc(s_arg, 1)
            x_high(0, 0, 0)
            x_high(0, 0, 1)
            act.wait_ge(s_ang, 1)
            flat = ang.rearrange("p k n -> p (k n)")
            act.activation(sn.rearrange("p k n -> p (k n)"), flat, ACT.Sin)
            act.activation(sh.rearrange("p k n -> p (k n)"), flat, ACT.Sin, scale=0.5).then_inc(s_sin, 1)
            act.wait_ge(s_lam, 1)
            copy(NX[:, SQ - 1, 0, :], lre[:, 0, :])
            copy(NX[:, SQ - 1, 1, :], lim[:, 0, :]).then_inc(s_xini, 1)

            def outer(n):
                act.wait_ge(s_nb, n + 1)
                copy(NB[:, half(n), 0, :], NB[:, half(n), 1, :]).then_inc(s_bdup, 1)
                copy(NB[:, half(n), 3, :], NB[:, half(n), 2, :]).then_inc(s_bdup, 1)

            def take(first, last):
                for t in range(first, last + 1):
                    if t not in BY_VECTOR:
                        filled(act, t)
                        copy(place(t), four(t)).then_inc(s_free[t % BANKS], 1)

            take(0, 1)
            outer(0)
            take(2, 3)
            act.wait_ge(s_lam, 2)
            copy(NR[:, :, 0, 0, :].bitcast(F32R), lim[:, R_POW:, :]).then_inc(s_rhi, 1)
            copy(NR[:, :, 0, 1, :].bitcast(F32R), lre[:, R_POW:, :]).then_inc(s_rhi, 1)
            act.activation(NR[:, :, 0, 2, :].bitcast(F32R), lim[:, R_POW:, :], ACT.Copy, scale=-1.0).then_inc(s_rhi, 1)
            take(4, 13)
            outer(1)
            take(14, T_END - 1)

            def x_odd(g, j):
                act.wait_ge(s_ulo[1], chan(g, j) + 1)
                copy(uod[j % 2][:], xt[1][:]).then_inc(s_uod, 1)

            def e_high(g, j):
                act.wait_ge(s_et, chan(g, j) + 1)
                copy(ehi[j % 2][:], e_bank(j)).then_inc(s_ehi, 1)

            def f_high(g, j):
                act.wait_ge(s_pf, chan(g, j) + 1)
                if exists(g, j, -2):
                    act.wait_ge(s_y, 2 * chan(g, j) - 2)
                copy(fhi[j % 2][:], pf[j % 2][:, 1, ::-1]).then_inc(s_fhi, 1)

            def t_high(g, j):
                act.wait_ge(s_t[j % 2], 16 * (chan(g, 0) // 2 + j // 2 + 1))
                copy(thi[j % 2][:], traw[j % 2][:, ::-1]).then_inc(s_thi, 1)

            def z_high(g, j, level):
                h = chan(g, j)
                if level:
                    act.wait_ge(s_l, 3 * h + level)
                else:
                    act.wait_ge(s_in, h + 1)
                a, b = (B * c for c in ZCOLS[level])
                copy(zhi[j % 2][:, a:b], vb[j % 2][:, a:b]).then_inc(s_zhi, 1)

            def slot(g, j):
                one, two = on(g, j, 1), on(g, j, 2)
                has1, has2 = exists(g, j, 1), exists(g, j, 2)
                if has1:
                    f_high(*one)
                    x_odd(*one)
                    z_high(*one, 0)
                    t_high(*one)
                    z_high(*one, 1)
                if has2:
                    e_high(*two)
                if has1:
                    z_high(*one, 2)
                if has2:
                    x_high(*two, 0)
                    x_high(*two, 1)
                if has1:
                    z_high(*one, 3)

            e_high(0, 0)
            slot(-1, SLOTS - 1)
            groups(act, slot)

        @block.vector
        def _(dve):
            done = [0]

            def link(ins):
                done[0] += 1
                ins.then_inc(s_dve, 1)
                dve.wait_ge(s_dve, done[0])

            def less(dst, src, high):
                return dve.tensor_tensor(dst, src, high.bitcast(F32), ALU.subtract)

            def x_low(g, j, par):
                dve.wait_ge(s_uhi[par], chan(g, j) + 1)
                less(ulo[j % 2][par][:], xt[par][:], uhi[j % 2][par][:]).then_inc(s_ulo[par], 1)

            LOG2E = 1.0 / math.log(2.0)
            LN2A = 0.693359375
            LN2B = math.log(2.0) - LN2A
            ROUND = 1.5 * 2.0 ** 23

            def reduced(step, k, r, src):
                if step == 0:
                    return dve.tensor_scalar(r, src, -87.0, 87.0, ALU.max, ALU.min)
                if step == 1:
                    return dve.tensor_scalar(k, r, LOG2E, ROUND, ALU.mult, ALU.add)
                if step == 2:
                    return dve.tensor_scalar(k, k, ROUND, None, ALU.subtract)
                part = LN2A if step == 3 else LN2B
                return dve.scalar_tensor_tensor(out=r, in0=k, scalar=-part, in1=r, op0=ALU.mult, op1=ALU.add)

            def series(q, k, r, two_k):
                dve.tensor_scalar(two_k.bitcast(I32), k, 127.0, float(2 ** 23), ALU.add, ALU.mult)
                link(dve.tensor_scalar(q, r, 1.0 / math.factorial(7), None, ALU.mult))
                for d in range(6, 0, -1):
                    link(dve.scalar_tensor_tensor(out=q, in0=q, scalar=1.0 / math.factorial(d), in1=r,
                                                  op0=ALU.add, op1=ALU.mult))

            def times_two_k(dst, q, two_k):
                return dve.scalar_tensor_tensor(out=dst, in0=q, scalar=1.0, in1=two_k, op0=ALU.add, op1=ALU.mult)

            def combine(lo, hi):
                m, s, f, re, im, t = (v[:, lo:hi, :] for v in (mag, sh, sn, lre, lim, view(q1)))
                link(dve.scalar_tensor_tensor(out=t, in0=s, scalar=-2.0, in1=s, op0=ALU.mult, op1=ALU.mult))
                dve.tensor_tensor(im, m, f, ALU.mult)
                link(dve.tensor_tensor(t, m, t, ALU.mult))
                dve.tensor_tensor(re, m, t, ALU.add).then_inc(s_lam, 1)

            dve.wait_ge(s_prm, 16 * 2)
            k, r, q = whole[:, 0:1 + N], q2[:, 0:1 + N], q3[:, 0:1 + N]
            for step in range(5):
                link(reduced(step, k, r, prm[:]))
            series(q, k, r, k)
            times_two_k(ex0[:], q, k).then_inc(s_ex0, 1)
            dve.wait_ge(s_ex0, 1)
            dve.wait_ge(s_ca, 16 * 2)
            dt = ex0[:, 0:1]
            dve.tensor_scalar(arg[:, 0, :], ex0[:, 1:1 + N], dt, -1.0, ALU.mult, ALU.mult).then_inc(s_arg, 1)
            link(dve.tensor_scalar(ang[:, 0, :], aim[:], dt, None, ALU.mult))
            for k in range(1, NPOW):
                ins = dve.tensor_scalar(ang[:, k, :], ang[:, 0, :], float(POWERS[k]), None, ALU.mult)
            link(ins)
            c1 = 6.28125
            c2 = round((2 * math.pi - c1) * 2 ** 21) / 2 ** 21
            c3 = 2 * math.pi - c1 - c2
            flat = ang.rearrange("p k n -> p (k n)")

            def reduced_angle(step):
                if step == 0:
                    return dve.tensor_scalar(q1[:], flat, 1.0 / (2 * math.pi), ROUND, ALU.mult, ALU.add)
                if step == 1:
                    return dve.tensor_scalar(q1[:], q1[:], ROUND, None, ALU.subtract)
                return dve.scalar_tensor_tensor(out=flat, in0=q1[:], scalar=-(c1, c2, c3)[step - 2], in1=flat,
                                                op0=ALU.mult, op1=ALU.add)

            def take_turns(ins):
                done[0] += 1
                ins.then_inc(s_dve, 1)
                dve.wait_ge(s_dve, done[0] - 1)

            n = len(POWERS[::2]) * N
            k, r, q, src = whole[:, 0:n], q2[:, 0:n], q3[:, 0:n], arg[:, 0:len(POWERS[::2]), :].rearrange("p k n -> p (k n)")
            for step in range(5):
                take_turns(reduced_angle(step))
                if step == 0:
                    dve.wait_ge(s_arg, len(POWERS[::2]))
                take_turns(reduced(step, k, r, src))
            link(dve.tensor_scalar(flat, flat, 3.1415925, -3.1415925, ALU.min, ALU.max))
            dve.engine_nop().then_inc(s_ang, 1)
            series(q, k, r, k)
            dve.wait_ge(s_norm, 1)
            dve.reciprocal(norm, norm)
            link(times_two_k(mag[:, 0:NPOW:2, :], q.rearrange("p (k n) -> p k n", n=N),
                             k.rearrange("p (k n) -> p k n", n=N)))
            dve.tensor_scalar(norm, norm, 2.0, None, ALU.mult).then_inc(s_norm, 1)
            link(dve.tensor_tensor(mag[:, 1:NPOW:2, :], mag[:, 0:NPOW - 1:2, :], mag[:, 0:NPOW - 1:2, :], ALU.mult))
            dve.wait_ge(s_sin, 1)
            combine(0, R_POW)
            link(dve.tensor_tensor(q[:, 0:N], q[:, 0:N], k[:, 0:N], ALU.mult))
            link(dve.scalar_tensor_tensor(out=em1[:], in0=k[:, 0:N], scalar=-1.0, in1=q[:, 0:N],
                                          op0=ALU.add, op1=ALU.add))
            dve.wait_ge(s_lam, 1)
            l1i = lim[:, 0, :]
            dve.wait_ge(s_g, 2)
            dve.tensor_tensor(t1, l1i, g_im, ALU.mult)
            dve.tensor_tensor(t3, l1i, g_re, ALU.mult)
            link(dve.tensor_tensor(l1r, em1[:], q1[:, 0:N], ALU.add))
            dve.tensor_tensor(t2, l1r, g_re, ALU.mult)
            link(dve.tensor_tensor(l1r, l1r, g_im, ALU.mult))
            dve.tensor_tensor(NY[:, SQ - 1, 1, :], t2, t1, ALU.add)
            link(dve.tensor_tensor(NY[:, SQ - 1, 0, :], t3, l1r, ALU.subtract))
            temps = [q1, q2, q3, q4]
            link(level(dve, link, NY, 1, 0, A_POW, temps, 0))
            link(level(dve, link, NY, 1, 0, A_POW, temps, 1))
            level(dve, link, NY, 1, 0, A_POW, temps, 2).then_inc(s_ny, 1)
            dve.wait_ge(s_ny, 1)
            minus(dve, NY, 0).then_inc(s_yneg, 1)
            level(dve, link, NY, 1, 0, A_POW, temps, 3).then_inc(s_ny, 1)
            dve.wait_ge(s_ny, 2)
            minus(dve, NY, 1).then_inc(s_yneg, 1)
            combine(R_POW, NPOW)
            dve.wait_ge(s_xini, 1)
            link(level(dve, link, NX, 0, 1, A_POW, temps, 0))
            link(level(dve, link, NX, 0, 1, A_POW, temps, 1))
            level(dve, link, NX, 0, 1, A_POW, temps, 2).then_inc(s_nx, 1)
            dve.wait_ge(s_nx, 1)
            minus(dve, NX, 0).then_inc(s_xneg, 1)
            level(dve, link, NX, 0, 1, A_POW, temps, 3, 0, XSPLIT).then_inc(s_nx, 1)
            dve.wait_ge(s_rhi, 3)
            for plane, src in ((0, lim), (1, lre)):
                dve.tensor_tensor(NR[:, :, 1, plane, :], src[:, R_POW:, :], NR[:, :, 0, plane, :],
                                  ALU.subtract).then_inc(s_rlo, 1)
            dve.tensor_tensor(NR[:, :, 1, 2, :], NR[:, :, 0, 0, :], lim[:, R_POW:, :], ALU.subtract).then_inc(s_rlo, 1)
            dve.wait_ge(s_nx, 2)
            dve.wait_ge(s_nxp, 1)
            minus(dve, NX, 1).then_inc(s_xneg, 1)
            dve.wait_ge(s_len, 48)
            dve.wait_ge(s_pool0, 1)
            dve.tensor_copy(flen[:], ilen[:])
            link(dve.tensor_reduce(dsel[:], ident[:, SQ - 1:P:SQ], mybir.AxisListType.X, ALU.add))
            link(dve.tensor_scalar(dall[:], dall[:], 1.0, dsel[:, 0:1], ALU.add, ALU.mult))

            def take(t):
                filled(dve, t)
                dve.tensor_copy(place(t), four(t)).then_inc(s_free[t % BANKS], 1)

            k0 = ksb[:].rearrange("p g (c i) -> p g c i", i=SQ)[:, :, :, SQ - 1]
            for t in BY_VECTOR:
                take(t)
                if t == T_K + 2:
                    for k in range(T_K, T_K + 4):
                        dve.wait_ge(s_free[k % BANKS], k // BANKS + 1)
                    dve.tensor_tensor(k0, k0, dall[:].rearrange("p (g c) -> p g c", c=8),
                                      ALU.add).then_inc(s_kfin, 1)
            x_low(0, 0, 0)
            x_low(0, 0, 1)
            for k in range(2):
                dve.memset(zhi[k][:, 0:B].bitcast(F32), 0.0)
                dve.memset(zlo[k][:, 0:B].bitcast(F32), 0.0)
            link(dve.tensor_scalar(mask[:], mask[:], flen[:, 0:1], None, ALU.is_lt))

            def e_low(g, j):
                dve.wait_ge(s_ehi, chan(g, j) + 1)
                less(elo[j % 2][:], e_bank(j), ehi[j % 2][:]).then_inc(s_elo, 1)

            def f_low(g, j):
                dve.wait_ge(s_fhi, chan(g, j) + 1)
                less(flo[j % 2][:], pf[j % 2][:, 1, ::-1], fhi[j % 2][:]).then_inc(s_flo, 1)

            def t_low(g, j):
                dve.wait_ge(s_thi, chan(g, j) + 1)
                less(tlo[j % 2][:], traw[j % 2][:, ::-1], thi[j % 2][:]).then_inc(s_tlo, 1)

            def z_low(g, j, level):
                a, b = (B * c for c in ZCOLS[level])
                dve.wait_ge(s_zhi, 4 * chan(g, j) + level + 1)
                less(zlo[j % 2][:, a:b], vb[j % 2][:, a:b], zhi[j % 2][:, a:b]).then_inc(s_zlo, 1)

            def choose(g, j, part):
                a = part * 512
                dve.copy_predicated(xs[j][:, a:a + 512], mask[:, a:a + 512], yb[j % 2][part][:]).then_inc(s_pred, 1)

            def slot(g, j):
                h = chan(g, j)
                one, two, back = on(g, j, 1), on(g, j, 2), on(g, j, -1)
                has1, has2, hasb = exists(g, j, 1), exists(g, j, 2), exists(g, j, -1)
                if hasb:
                    dve.wait_ge(s_y, 2 * h)
                if has1:
                    f_low(*one)
                if hasb:
                    choose(*back, 0)
                if has1:
                    z_low(*one, 0)
                if hasb:
                    choose(*back, 1)
                if has1:
                    t_low(*one)
                    z_low(*one, 1)
                if has2:
                    e_low(*two)
                if has1:
                    z_low(*one, 2)
                if has2:
                    x_low(*two, 0)
                    x_low(*two, 1)
                if has1:
                    z_low(*one, 3)

            e_low(0, 0)
            slot(-1, SLOTS - 1)
            groups(dve, slot)
            for part in range(2):
                dve.wait_ge(s_y, 2 * H - 1 + part)
                choose((H - 1) // SLOTS, (H - 1) % SLOTS, part)

        @block.tensor
        def _(pe):
            pe.wait_ge(s_pool0, 1)

            def keep_warm(n, bank):
                for _ in range(n):
                    pe.transpose(bank[:, 0:P], ident[:], ident[:])

            def turn_x(g, j, par):
                pe.wait_ge(s_x[j], 32 * (g + 1))
                for c in range(CPH):
                    b = 2 * c + par
                    mm = pe.transpose(xt[par][:, c * P:(c + 1) * P], xs[j][:, b * BLK:(b + 1) * BLK], ident[:])
                mm.then_inc(s_tr, 1)

            def turn_e(g, j):
                pe.wait_ge(s_pf, chan(g, j) + 1)
                if exists(g, j, -3):
                    pe.wait_ge(s_pred, 2 * chan(g, j) - 4)
                pe.transpose(e_bank(j)[:, 0:P], pf[j % 2][:, 0, 0:P], ident[:])
                pe.transpose(e_bank(j)[:, P:2 * P], pf[j % 2][:, 0, P:2 * P], ident[:]).then_inc(s_et, 1)

            def three(o, a_hi, a_lo, b_hi, b_lo, start, stop):
                pe.matmul(o, a_hi, b_hi, start=start, stop=False, skip_group_check=True)
                pe.matmul(o, a_hi, b_lo, start=False, stop=False, skip_group_check=True)
                return pe.matmul(o, a_lo, b_hi, start=False, stop=stop, skip_group_check=True)

            def chunk_sums(g, j):
                h, k = chan(g, j), j % 2
                cols = slice(0, (NC - 1) * B)
                pe.wait_ge(s_elo, h + 1)
                if exists(g, j, -2):
                    pe.wait_ge(s_zlo, 4 * h - 4)
                for par in range(2):
                    pe.wait_ge(s_ulo[par], h + 1)
                    e = slice(par * P, (par + 1) * P)
                    mm = three(vb[k][:, B:NC * B], ehi[k][:, e], elo[k][:, e], uhi[k][par][:, cols],
                               ulo[k][par][:, cols], par == 0, False)
                mm.then_inc(s_in, 1)

            def hop(g, j, level):
                h, k = chan(g, j), j % 2
                if level == 0:
                    pe.wait_ge(s_r, h + 1)
                pe.wait_ge(s_zlo, 4 * h + level + 1)
                a, b, by = HOPS[level]
                w = [rot[k][:, 4 * level + 2 * i:4 * level + 2 * i + 2, :].rearrange("p c n -> p (c n)")
                     for i in range(2)]
                cols = slice(B * a, B * b)
                three(vb[k][:, B * (a + by):B * (b + by)], w[0], w[1], zhi[k][:, cols], zlo[k][:, cols], False,
                      level == 2).then_inc(s_l, 1)

            def y_cols(g, j, c):
                return yb[j % 2][c // 2][:, (c % 2) * CHUNK:(c % 2 + 1) * CHUNK]

            def toep_even(g, j, c):
                k, b = j % 2, slice(c * P, (c + 1) * P)
                if c == 0:
                    pe.wait_ge(s_tlo, chan(g, j) + 1)
                    if exists(g, j, -2):
                        pe.wait_ge(s_pred, 2 * chan(g, j) - 2)
                three(y_cols(g, j, c), uhi[k][0][:, b], ulo[k][0][:, b], thi[k][:], tlo[k][:], c % 2 == 0, False)

            def toep_odd(g, j, c):
                k, b = j % 2, slice(c * P, (c + 1) * P)
                if c == 0:
                    pe.wait_ge(s_uod, chan(g, j) + 1)
                mm = pe.matmul(y_cols(g, j, c)[:, BLK:2 * BLK], uod[k][:, b], traw[k][:, :BLK - 1:-1], start=False,
                               stop=False, skip_group_check=True)
                if c == CPH - 1:
                    mm.then_inc(s_intra, 1)

            def from_state(g, j, c):
                k, b = j % 2, slice(c * P, (c + 1) * P)
                if c == 0:
                    pe.wait_ge(s_flo, chan(g, j) + 1)
                    pe.wait_ge(s_zlo, 4 * chan(g, j) + 4)
                mm = three(y_cols(g, j, c), zhi[k][:, b], zlo[k][:, b], fhi[k][:], flo[k][:], False, c % 2 == 1)
                if c % 2:
                    mm.then_inc(s_y, 1)

            def slot(g, j):
                here, one, two = (g, j), on(g, j, 1), on(g, j, 2)
                has0, has1, has2 = exists(g, j, 0), exists(g, j, 1), exists(g, j, 2)
                if has1:
                    chunk_sums(*one)
                if not has0:
                    keep_warm(WARM_SCAN, vb[1])
                if has0 and exists(g, j, -1):
                    toep_even(*here, 0)
                    toep_odd(*here, 0)
                    toep_even(*here, 1)
                    toep_odd(*here, 1)
                    toep_even(*here, 2)
                if has0 and not exists(g, j, -1):
                    toep_even(*here, 3)
                if has1:
                    hop(*one, 0)
                if has0 and exists(g, j, -1):
                    toep_odd(*here, 2)
                    toep_even(*here, 3)
                if has0:
                    toep_odd(*here, 3)
                if has2:
                    turn_e(*two)
                    turn_x(*two, 0)
                if not has0:
                    toep_even(*one, 0)
                    toep_odd(*one, 0)
                if has1:
                    hop(*one, 1)
                if has2:
                    turn_x(*two, 1)
                if not has0:
                    toep_even(*one, 1)
                    toep_odd(*one, 1)
                if has0:
                    from_state(*here, 0)
                    from_state(*here, 1)
                if has1:
                    hop(*one, 2)
                if not has0:
                    pe.wait_ge(s_elo, chan(*two) + 1)
                    toep_even(*one, 2)
                    toep_odd(*one, 2)
                if has0:
                    from_state(*here, 2)
                    from_state(*here, 3)

            natural = {"Y1": (NY, 1), "Y2": (NY, 0), "X1": (NX, 0), "X2": (NX, 1), "B1": (NB, 0), "B2": (NB, 2),
                       "bsel": (NB, 1)}

            def turn(first, last):
                for t in range(first, last + 1):
                    name, i = STEPS[t]
                    if t >= BANKS:
                        pe.wait_ge(s_free[t % BANKS], t // BANKS)
                    for r in range(4):
                        if name == "R":
                            src = NR[:, i // 4, r // 2, 1 - r % 2:3 - r % 2, :]
                        else:
                            table, plane = natural[name]
                            src = table[:, i + r, plane:plane + 2, :]
                        mm = pe.transpose(pro[t % BANKS][:, r * P:(r + 1) * P], src.rearrange("p c n -> p (c n)"),
                                          ident[:])
                    mm.then_inc(s_fill[t % BANKS], 1)

            turn_x(0, 0, 0)
            turn_x(0, 0, 1)

            pe.wait_ge(s_lam, 1)
            keep_warm(WARM_TABLES, pro[BANKS - 1])
            pe.wait_ge(s_yneg, 1)
            turn(0, 1)
            pe.wait_ge(s_nb, 1)
            turn(2, 3)
            pe.wait_ge(s_yneg, 2)
            turn(4, 5)
            pe.wait_ge(s_bdup, 2)
            turn(6, 13)
            pe.wait_ge(s_nb, 2)
            turn(14, 15)
            pe.wait_ge(s_xneg, 1)
            turn(16, 19)
            pe.wait_ge(s_bdup, 4)
            turn(20, 23)
            for t in (T_BSEL - 1, T_BSEL):
                pe.wait_ge(s_free[t % BANKS], t // BANKS + 1)
            for g in range(H // 8):
                t = T_K + g // 4
                if g % 4 == 0:
                    pe.wait_ge(s_free[t % BANKS], t // BANKS)
                mm = pe.matmul(pro[t % BANKS][:, (g % 4) * P:(g % 4 + 1) * P],
                               W1[:, 1, 8 * g:8 * g + 8, :].rearrange("p c i -> p (c i)"),
                               bsel[:, 8 * g:8 * g + 8, :].rearrange("p c i -> p (c i)"), start=True, stop=True)
                if g % 4 == 3:
                    mm.then_inc(s_fill[t % BANKS], 1)
            pe.wait_ge(s_xneg, 2)
            turn(T_K + 4, T_R - 1)
            pe.wait_ge(s_rlo, 3)
            turn(T_R, T_END - 1)
            for t in range(T_END - BANKS, T_END):
                pe.wait_ge(s_free[t % BANKS], t // BANKS + 1)
            keep_warm(WARM_LOOP, vb[1])
            turn_e(0, 0)
            slot(-1, SLOTS - 1)
            groups(pe, slot)


_INS = ['x', 'itok_B_8_3872', 'L0_cond_log_dt', 'L0_cond_C', 'L0_cond_log_A_real', 'L0_cond_A_imag', 'L0_cond_D']


def kernel(**inputs):
    import numpy as _np
    import concourse.bacc as _bacc
    from concourse import mybir as _mybir
    from concourse.bass_utils import run_bass_kernel_spmd as _run

    nc = _bacc.Bacc("TRN2", target_bir_lowering=False, num_devices=1)
    arrays, args = {}, []
    for name in _INS:
        a = _np.ascontiguousarray(inputs[name])
        arrays[f"in_{name}_dram"] = a
        args.append(nc.dram_tensor(f"in_{name}_dram", a.shape, _mybir.dt.from_np(a.dtype), kind="ExternalInput").ap())
    out = nc.dram_tensor("out_0_dram", inputs["x"].shape, _mybir.dt.float32, kind="ExternalOutput").ap()
    s4d_kernel(nc, *args, out)
    r = _run(nc, [arrays], core_ids=[0])
    return r.results[0]["out_0_dram"]
```
